# Optimizing a Trainium2 kernel written in Bass

```python
import numpy as np
import jax
import jax.numpy as jnp

def _softmax(x, axis=-1):
    return jax.nn.softmax(x, axis=axis)

def _gelu(x):
    return jax.nn.gelu(x, approximate=True)

def _silu(x):
    return jax.nn.silu(x)

def _sigmoid(x):
    return jax.nn.sigmoid(x)

def _layernorm(x, axis=-1, eps=1e-05):
    m = jnp.mean(x, axis=axis, keepdims=True)
    v = jnp.var(x, axis=axis, keepdims=True)
    return (x - m) / jnp.sqrt(v + eps)

def _scatter_add(tgt, idx, src, axis=0):
    return tgt.at[idx].add(src)

def _segment_sum(src, seg, n):
    return jax.ops.segment_sum(src, seg, n)
kernel_name = 'mk_gnn_preln_d4_gnn_r8_df7e54'

def setup_inputs(seed: int=0):
    np.random.seed(seed)
    _w = jnp.asarray

    def _rec_inputs():
        import jax
        import jax.numpy as jnp
        _gk = jax.random.key(seed)
        x = -0.000202 + 1 * jax.random.normal(jax.random.fold_in(_gk, 1), (12500, 64), jnp.float32)
        src = jax.random.randint(jax.random.fold_in(_gk, 2), (400000,), 0, 12500, jnp.int32)
        dst = jax.random.randint(jax.random.fold_in(_gk, 3), (400000,), 0, 12500, jnp.int32)
        _o = jnp.argsort(dst, stable=True)
        src = src[_o]
        dst = dst[_o]
        edge_attr_64 = -8.16379e-05 + 0.999858 * jax.random.normal(jax.random.fold_in(_gk, 12), (400000, 64), jnp.float32)
        edge_weight = jax.random.uniform(jax.random.fold_in(_gk, 14), (400000,), jnp.float32, 0.0, 1)
        edge_weight_n2 = jax.random.uniform(jax.random.fold_in(_gk, 15), (400000,), jnp.float32, 0.0, 1)
        return (x, src, dst, edge_attr_64, edge_weight, edge_weight_n2)
    x, src, dst, edge_attr_64, edge_weight, edge_weight_n2 = _rec_inputs()

    def _L0_gnn_setup():
        import jax, jax.numpy as jnp
        import numpy as np
        N = 12500
        E = 200000
        H = 64
        key = jax.random.key(seed)
        k1, k2, k3, k4, k5 = jax.random.split(key, 5)
        x = jax.random.normal(k1, (N, H), dtype=jnp.float32)
        src = jax.random.randint(k2, (E,), 0, N, dtype=jnp.int32)
        off = jax.random.randint(k3, (E,), 1, N, dtype=jnp.int32)
        dst = (src + off) % N
        edge_index = jnp.stack([src, dst])
        w_i = jax.random.normal(k4, (H,), dtype=jnp.float32) / np.sqrt(H)
        w_j = jax.random.normal(k5, (H,), dtype=jnp.float32) / np.sqrt(H)
        return {'x': x, 'edge_index': edge_index, 'w_i': w_i, 'w_j': w_j}
    _L0_gnn_all = _L0_gnn_setup()
    _L0_gnn_in = {k: v for k, v in _L0_gnn_all.items() if k in ('w_i', 'w_j')}
    del _L0_gnn_all

    def _L1_gnn_setup():
        import jax, jax.numpy as jnp
        import numpy as np
        N_NODES = 12500
        N_EDGES = 200000
        D_FEAT = 64
        key = jax.random.key(seed)
        k1, k2 = jax.random.split(key)
        x = jax.random.normal(k1, (N_NODES, D_FEAT), dtype=jnp.float32)
        edge_index = jax.random.randint(k2, (2, N_EDGES), 0, N_NODES, dtype=jnp.int64)
        return {'x': x, 'edge_index': edge_index}
    _L1_gnn_all = _L1_gnn_setup()
    _L1_gnn_in = {k: v for k, v in _L1_gnn_all.items() if k in ()}
    del _L1_gnn_all

    def _L2_gnn_setup():
        import jax, jax.numpy as jnp
        import numpy as np
        NUM_NODES = 12500
        EMBED_DIM = 64
        NUM_EDGES = 156250
        NUM_LAYERS = 3
        key = jax.random.key(seed)
        k1, k2 = jax.random.split(key)
        edge_index = jax.random.randint(k1, (2, NUM_EDGES), 0, NUM_NODES, dtype=jnp.int32)
        emb = 0.1 * jax.random.normal(k2, (NUM_NODES, EMBED_DIM), dtype=jnp.float32)
        return {'edge_index': edge_index, 'emb': emb}
    _L2_gnn_all = _L2_gnn_setup()
    _L2_gnn_in = {k: v for k, v in _L2_gnn_all.items() if k in ()}
    del _L2_gnn_all

    def _L3_gnn_setup():
        import jax, jax.numpy as jnp
        import numpy as np
        N_NODES = 12500
        N_PAIRS = 200000
        F = 64
        H = 4
        D = F // H
        key = jax.random.key(seed)
        ks = jax.random.split(key, 9)
        x = jax.random.normal(ks[0], (N_NODES, F), dtype=jnp.float32)
        w_ij = jax.random.normal(ks[1], (N_PAIRS, F), dtype=jnp.float32)
        phi_r_cut = jax.random.uniform(ks[2], (N_PAIRS,), dtype=jnp.float32)
        pair_mask = jnp.ones((N_PAIRS,), dtype=jnp.float32)
        Wq = jax.random.normal(ks[3], (H, D, D), dtype=jnp.float32) / np.sqrt(D)
        Wk = jax.random.normal(ks[4], (H, D, D), dtype=jnp.float32) / np.sqrt(D)
        Wv = jax.random.normal(ks[5], (H, D, D), dtype=jnp.float32) / np.sqrt(D)
        idx_i = jnp.sort(jax.random.randint(ks[6], (N_PAIRS,), 0, N_NODES)).astype(jnp.int64)
        idx_j = jax.random.randint(ks[7], (N_PAIRS,), 0, N_NODES).astype(jnp.int64)
        return {'x': x, 'w_ij': w_ij, 'phi_r_cut': phi_r_cut, 'pair_mask': pair_mask, 'Wq': Wq, 'Wk': Wk, 'Wv': Wv, 'idx_i': idx_i, 'idx_j': idx_j}
    _L3_gnn_all = _L3_gnn_setup()
    _L3_gnn_in = {k: v for k, v in _L3_gnn_all.items() if k in ('Wq', 'Wk', 'Wv')}
    del _L3_gnn_all
    return {'x': x, 'src': src, 'dst': dst, 'edge_attr_64': edge_attr_64, 'edge_weight': edge_weight, 'edge_weight_n2': edge_weight_n2, 'L0_gnn_w_i': _L0_gnn_in['w_i'], 'L0_gnn_w_j': _L0_gnn_in['w_j'], 'L3_gnn_Wq': _L3_gnn_in['Wq'], 'L3_gnn_Wk': _L3_gnn_in['Wk'], 'L3_gnn_Wv': _L3_gnn_in['Wv']}

def reference(x, src, dst, edge_attr_64, edge_weight, edge_weight_n2, L0_gnn_w_i, L0_gnn_w_j, L3_gnn_Wq, L3_gnn_Wk, L3_gnn_Wv):
    import jax
    import jax.numpy as jnp

    def _L0_gnn_ref(x, edge_index, w_i, w_j):
        import jax, jax.numpy as jnp
        import numpy as np
        N = 12500
        E = 200000
        H = 64
        n = x.shape[0]
        loops = jnp.arange(n, dtype=edge_index.dtype)
        src = jnp.concatenate([edge_index[0], loops])
        dst = jnp.concatenate([edge_index[1], loops])
        s_i = x @ w_i
        s_j = x @ w_j
        e = jax.nn.leaky_relu(s_i[dst] + s_j[src], 0.01)
        e_max = jax.ops.segment_max(e, dst, num_segments=n)
        e_exp = jnp.exp(e - e_max[dst])
        denom = jax.ops.segment_sum(e_exp, dst, num_segments=n)
        alpha = e_exp / denom[dst]
        out = jax.ops.segment_sum(alpha[:, None] * x[src], dst, num_segments=n)
        return jax.nn.relu(out)

    def _L1_gnn_ref(x, edge_index):
        import jax, jax.numpy as jnp
        import numpy as np
        N_NODES = 12500
        N_EDGES = 200000
        D_FEAT = 64
        N = x.shape[0]
        row, col = (edge_index[0], edge_index[1])
        w = jnp.where(row != col, jnp.ones((), x.dtype), jnp.zeros((), x.dtype))
        loop = jnp.arange(N, dtype=row.dtype)
        row_a = jnp.concatenate([row, loop])
        col_a = jnp.concatenate([col, loop])
        w_a = jnp.concatenate([w, jnp.ones((N,), x.dtype)])
        deg = jax.ops.segment_sum(w_a, row_a, num_segments=N)
        dinv = jnp.where(deg > 0, jax.lax.rsqrt(deg), jnp.zeros((), x.dtype))
        norm = dinv[row_a] * w_a * dinv[col_a]
        out = jax.ops.segment_sum(norm[:, None] * x[col_a], row_a, num_segments=N)
        return out

    def _L2_gnn_ref(edge_index, emb):
        import jax, jax.numpy as jnp
        import numpy as np
        NUM_NODES = 12500
        EMBED_DIM = 64
        NUM_EDGES = 156250
        NUM_LAYERS = 3
        n = emb.shape[0]
        row, col = (edge_index[0], edge_index[1])
        deg = jax.ops.segment_sum(jnp.ones((row.shape[0],), emb.dtype), col, num_segments=n)
        deg_inv_sqrt = jnp.where(deg > 0, jax.lax.rsqrt(jnp.maximum(deg, 1.0)), 0.0).astype(emb.dtype)
        norm = deg_inv_sqrt[row] * deg_inv_sqrt[col]
        x = emb
        acc = emb
        for _ in range(NUM_LAYERS):
            msgs = norm[:, None] * x[row]
            x = jax.ops.segment_sum(msgs, col, num_segments=n)
            acc = acc + x
        return acc / (NUM_LAYERS + 1)

    def _L3_gnn_ref(x, w_ij, phi_r_cut, pair_mask, Wq, Wk, Wv, idx_i, idx_j):
        import jax, jax.numpy as jnp
        import numpy as np
        N_NODES = 12500
        N_PAIRS = 200000
        F = 64
        H = 4
        D = F // H
        n, f = x.shape
        h, d, _ = Wq.shape
        xh = x.reshape(n, h, d)
        wh = w_ij.reshape(-1, h, d)
        q_i = jnp.einsum('nhd,hde->nhe', xh, Wq)[idx_i]
        k_j = jnp.einsum('nhd,hde->nhe', xh, Wk)[idx_j]
        alpha = (q_i * wh * k_j).sum(axis=-1) / jnp.sqrt(jnp.asarray(d, x.dtype))
        alpha = alpha * (pair_mask * phi_r_cut)[:, None]
        v_j = jnp.einsum('nhd,hde->nhe', xh, Wv)[idx_j]
        out = jax.ops.segment_sum(alpha[..., None] * v_j, idx_i, num_segments=n)
        return out.reshape(n, f)
    edge_index = jnp.stack([src, dst])
    h = jnp.maximum(_layernorm(x, axis=-1), 0.0)
    x = x + _L0_gnn_ref(h, edge_index, L0_gnn_w_i, L0_gnn_w_j)
    h = jnp.maximum(_layernorm(x, axis=-1), 0.0)
    x = x + _L1_gnn_ref(h, edge_index)
    h = jnp.maximum(_layernorm(x, axis=-1), 0.0)
    x = x + _L2_gnn_ref(edge_index, h)
    h = jnp.maximum(_layernorm(x, axis=-1), 0.0)
    x = x + _L3_gnn_ref(h, edge_attr_64, edge_weight, edge_weight_n2, L3_gnn_Wq, L3_gnn_Wk, L3_gnn_Wv, src, dst)
    return x

_drawn_inputs = setup_inputs


def setup_inputs(seed=0):
    import zlib

    import numpy as np

    out = dict(_drawn_inputs(seed))
    spreads = {}
    factors = {}
    for name, (base, spread) in spreads.items():
        noise = np.random.default_rng([zlib.crc32(name.encode()), seed]).standard_normal(out[name].shape)
        drawn = base * np.exp(spread * noise) if base else spread * noise
        out[name] = jnp.asarray(drawn.astype(out[name].dtype))
    for name, factor in factors.items():
        out[name] = (out[name] * factor).astype(out[name].dtype)
    return out
```

```python
from contextlib import ExitStack

import concourse.bass as bass
from concourse import mybir

ALU = mybir.AluOpType
ACT = mybir.ActivationFunctionType
F32 = mybir.dt.float32
BF16 = mybir.dt.bfloat16
I32 = mybir.dt.int32
AX = mybir.AxisListType

P = 128
HUGE = 1.0e30


def gnn_four_layers(nc, x, src, dst, edge_attr, edge_weight, edge_weight2, w_i, w_j, Wq, Wk, Wv, out):
    N, F = x.shape
    E = src.shape[0]
    HEADS, D, _ = Wq.shape
    EPS = 1e-5
    NBLK = -(-N // P)
    REST = N - (NBLK - 1) * P
    ROWS = NBLK * P

    JT = 2
    GROUP = JT * P
    PT, PG = 8, 4
    NPART = 4
    most = E // GROUP + NBLK
    ITERS = -(-most // (NPART * PG))
    NG = ITERS * NPART * PG
    SLOTS = NG * GROUP
    RA = F + 4
    A_LO, A_LON, A_PHI, A_IDX = F, F + 1, F + 2, F + 3
    RB = 2

    T = E // P
    SC = 5
    CHUNKS = 5
    TURNS = T // (SC * CHUNKS)
    assert T * P == E and TURNS * SC * CHUNKS == T and D * HEADS == F

    fileA = nc.dram_tensor("fileA", (SLOTS, RA), F32, kind="Internal").ap()
    fileB = nc.dram_tensor("fileB", (SLOTS, RB), F32, kind="Internal").ap()
    blkfile = nc.dram_tensor("blkfile", (2, NG), I32, kind="Internal").ap()
    TABW = [F + 1, F, F, F, F, 2 * F]
    table = [nc.dram_tensor(f"table{l}", (ROWS, w), F32, kind="Internal").ap() for l, w in enumerate(TABW)]

    with ExitStack() as ctx:
        def sb(name, shape, dt=F32):
            return ctx.enter_context(nc.sbuf_tensor(name, shape, dt))

        def sem(name):
            return ctx.enter_context(nc.semaphore(name))

        iota_i = sb("iota_i", [P, P], I32)
        part_i = sb("part_i", [P, 1], I32)
        iota = sb("iota", [P, P])
        part = sb("part", [P, 1])
        iota_b = sb("iota_b", [P, P], BF16)
        ident = sb("ident", [P, P])
        before = sb("before", [P, P], BF16)
        upto = sb("upto", [P, P], BF16)
        ones_b = sb("ones_b", [P, P], BF16)
        blkrow = sb("blkrow", [1, 2, NG], I32)
        blk_i = sb("blk_i", [P, 2, NG // P], I32)
        wcols = sb("wcols", [P, 2, F])
        Wqk = sb("Wqk", [P, 2, 2, F])
        Wvb = sb("Wvb", [P, 2, F])
        degs = sb("degs", [P, 2, NBLK])
        dinv1 = sb("dinv1", [P, NBLK])
        dinv2 = sb("dinv2", [P, NBLK])
        stat = sb("stat", [P, 4, NBLK])
        start = sb("start", [P, 2, NBLK])
        start_r = sb("start_r", [P, 2, NBLK])
        start_rows = start_r[:, :, :].rearrange("p k b -> p (k b)")
        cntf = sb("cntf", [P, 2, NBLK])
        cnti = sb("cnti", [P, 2, NBLK], I32)
        gnum = sb("gnum", [P, NG // P])
        gnum_i = sb("gnum_i", [P, NG // P], I32)
        zeros_b = sb("zeros_b", [P, 512], BF16)

        BIG = NBLK * F
        area = sb("area", [P, 5 * BIG])
        x_sb = area[:, 0:BIG].rearrange("p (b f) -> p b f", f=F)
        h_sb = area[:, BIG:2 * BIG].rearrange("p (b f) -> p b f", f=F)
        acc = area[:, 2 * BIG:3 * BIG].rearrange("p (b f) -> p b f", f=F)
        tmp = area[:, 3 * BIG:4 * BIG].rearrange("p (b f) -> p b f", f=F)
        q_sb = area[:, 4 * BIG:5 * BIG].rearrange("p (b f) -> p b f", f=F)

        hs = area[:, 3 * BIG:3 * BIG + NBLK * (F + 1)].rearrange("p (b f) -> p b f", f=F + 1)

        cut = [0]

        def carve(n):
            a = area[:, cut[0]:cut[0] + n]
            cut[0] += n
            return a
        srcI = carve(T).bitcast(I32)
        dstI = carve(T).bitcast(I32)
        phi = carve(T)
        phi2 = carve(T)
        TB = T + 1
        keys = carve(2 * TB // 2 + 1).bitcast(BF16)[:, 0:2 * TB].rearrange("p (k t) -> p k t", k=2)
        los = carve(3 * TB // 2 + 1).bitcast(BF16)[:, 0:3 * TB].rearrange("p (k t) -> p k t", k=3)
        FILL = NG * JT // 64
        fillA = carve(FILL * RA).rearrange("p (r c) -> p r c", c=RA)
        fillB = carve(FILL * RB).rearrange("p (r c) -> p r c", c=RB)
        work_i = carve(T).bitcast(I32)
        assert cut[0] <= 5 * BIG and FILL * 64 == NG * JT

        oh_area = sb("oh_area", [P, 3 * PT * P + P])
        ohkey = sb("ohkey", [P, CHUNKS, SC, 2, NBLK], BF16)
        ohlo = oh_area[:, 0:CHUNKS * SC * P].bitcast(BF16).rearrange("p (c t k n) -> p c t k n", c=CHUNKS, t=SC, k=2)
        pos = sb("pos", [P, CHUNKS, SC, 2])
        posI = sb("posI", [P, CHUNKS, SC, 2], I32)
        trash = sb("trash", [P, 2, NBLK])
        rowB = sb("rowB", [P, CHUNKS, SC, RB])
        rec_area = sb("rec_area", [P, NPART * PT * RA])
        rowA = rec_area[:, 0:CHUNKS * SC * RA].rearrange("p (c t w) -> p c t w", c=CHUNKS, t=SC)
        rec = rec_area[:, :].rearrange("p (q t w) -> p q t w", q=NPART, t=PT)
        recB = sb("recB", [P, NPART, PT, RB])
        gat = sb("gat", [P, NPART, PT, 2 * F])
        oh = oh_area[:, 0:2 * PT * P].rearrange("p (r t n) -> p r t n", r=2, t=PT)
        mask, probs = oh[:, 0, :, :], oh[:, 1, :, :]
        ohT = oh_area[:, 2 * PT * P:3 * PT * P].rearrange("p (t n) -> p t n", t=PT)
        sc = sb("sc", [P, PT * P])
        sic = sb("sic", [P, PG])
        gmax = sb("gmax", [P, PG])
        lowest = sb("lowest", [P, PG])
        fall = sb("fall", [P, PG])
        fac = sb("fac", [P, PG])
        rsum = sb("rsum", [P, PG])
        msg = sc[:, 0:PT * F].rearrange("p (t f) -> p t f", t=PT)
        msg2 = sc[:, PT * F:2 * PT * F].rearrange("p (t f) -> p t f", t=PT)
        alpha = sb("alpha", [P, PT, HEADS])
        two = sb("two", [P, 2 * F])
        hT = sb("hT", [P, 2 * F])

        bank = [ctx.enter_context(nc.psum_tensor(f"bank{b}", [P, 512], F32)) for b in range(8)]

        def sems(name, n):
            return [sem(f"{name}{k}") for k in range(n)]

        s_iota = sem("s_iota")
        s_in = sem("s_in")
        s_xin = sem("s_xin")
        s_x0 = sem("s_x0")
        s_win = sem("s_win")
        s_w0 = sem("s_w0")
        s_const = sem("s_const")
        s_fillsrc = sem("s_fillsrc")
        s_fill = sem("s_fill")
        s_dve = sem("s_dve")
        s_ckey = sems("s_ckey", CHUNKS)
        s_cnt = sems("s_cnt", CHUNKS)
        s_start = sem("s_start")
        s_blki = sem("s_blki")
        s_blk = sem("s_blk")
        s_skey = sems("s_skey", CHUNKS)
        s_rank = sem("s_rank")
        s_read = sem("s_read")
        s_chunk = sems("s_chunk", CHUNKS)
        s_rows = sems("s_rows", CHUNKS)
        s_wld = sems("s_wld", CHUNKS)
        s_posf = sem("s_posf")
        s_pos = sems("s_pos", CHUNKS)
        s_go = sem("s_go")
        s_sc = sems("s_sc", CHUNKS)
        s_rec = sems("s_rec", NPART)
        s_gat = [sems("s_gat_early", NPART), sems("s_gat_late", NPART)]
        s_freed = sems("s_freed", NPART)
        s_var = sem("s_var")
        s_root = sem("s_root")
        s_y = sem("s_y")
        s_tab = sem("s_tab")
        s_oh = sem("s_oh")
        s_agg = sem("s_agg")
        s_acc = sem("s_acc")
        s_msk = sem("s_msk")
        s_zt = sem("s_zt")
        s_sic = sem("s_sic")
        s_t = sem("s_t")
        s_l = sem("s_l")
        s_low = sem("s_low")
        s_p = sem("s_p")
        s_pt = sem("s_pt")
        s_ptc = sem("s_ptc")
        s_oT = sem("s_oT")
        s_oTc = sem("s_oTc")
        s_qg = sem("s_qg")
        s_m = sem("s_m")
        s_msg = sem("s_msg")
        s_two = sem("s_two")
        s_tr = sem("s_tr")
        s_trc = sem("s_trc")
        s_pr = sem("s_pr")
        s_prc = sem("s_prc")
        s_accd = sem("s_accd")
        s_out = sem("s_out")

        block = ctx.enter_context(nc.Block())

        PASSES = ["B", "A", "B", "B", "B", "A"]
        LAST = len(PASSES) - 1
        NPP = ITERS * NPART
        LOADS = [16 * (JT if l == 1 else 1) for l in range(len(PASSES))]
        LOADED = [sum(LOADS[:l]) * ITERS for l in range(len(PASSES))]
        fileA_v = fileA.rearrange("(g p j) c -> p g j c", p=P, j=JT)
        fileB_v = fileB.rearrange("(g p j) c -> p g j c", p=P, j=JT)

        def turns(eng, count, body, first=1, last=0):
            for i in range(first):
                body(i)
            with eng.Fori(first, count - last) as i:
                body(i)
            for i in range(count - last, count):
                body(i)

        def isfirst(i):
            return isinstance(i, int) and i == 0

        def islast(i):
            return isinstance(i, int) and i == ITERS - 1

        def node_rows(t):
            return t.rearrange("(b p) f -> p b f", p=P)

        @block.sync
        def _(sp):
            sp.dma_start(srcI, src.rearrange("(p t) -> p t", p=P)).then_inc(s_in, 16)
            sp.dma_start(dstI, dst.rearrange("(p t) -> p t", p=P)).then_inc(s_in, 16)
            sp.dma_start(phi, edge_weight.rearrange("(p t) -> p t", p=P)).then_inc(s_in, 16)
            sp.dma_start(phi2, edge_weight2.rearrange("(p t) -> p t", p=P)).then_inc(s_in, 16)
            sp.dma_start(wcols[:, 0, :], w_i.partition_broadcast(P)).then_inc(s_in, 16)
            sp.dma_start(wcols[:, 1, :], w_j.partition_broadcast(P)).then_inc(s_in, 16)
            sp.wait_ge(s_fillsrc, 1)
            fA = fileA.rearrange("(k p r) c -> k p r c", p=P, r=FILL)
            fB = fileB.rearrange("(k p r) c -> k p r c", p=P, r=FILL)
            for k in range(SLOTS // (P * FILL)):
                sp.dma_start(fA[k], fillA).then_inc(s_fill, 16)
                sp.dma_start(fB[k], fillB).then_inc(s_fill, 16)
            sp.wait_ge(s_w0, 1)
            for b in range(2):
                for hd in range(HEADS):
                    rows = slice(b * F + hd * D, b * F + hd * D + D)
                    cols = slice(hd * D, hd * D + D)
                    sp.dma_start(Wqk[rows, b, 0, cols], Wq[hd]).then_inc(s_win, 16)
                    sp.dma_start(Wqk[rows, b, 1, cols], Wk[hd]).then_inc(s_win, 16)
                    sp.dma_start(Wvb[rows, b, cols], Wv[hd]).then_inc(s_win, 16)
            ea = edge_attr.rearrange("(p t) f -> p t f", p=P)
            def load_chunks(i):
                for c in range(CHUNKS):
                    if not isfirst(i):
                        sp.wait_ge(s_sc[c], i * (2 * SC * 16))
                    sp.dma_start(rowA[:, c, :, 0:F], ea[:, bass.ds(i * (SC * CHUNKS) + c * SC, SC), :]).then_inc(s_wld[c], 16)

            turns(sp, TURNS, load_chunks)
            for c in range(CHUNKS):
                sp.wait_ge(s_sc[c], TURNS * 2 * SC * 16)
            sp.wait_ge(s_blki, 1)
            for k in range(2):
                sp.dma_start(blkfile[k:k + 1, :].rearrange("o (p j) -> (o p) j", p=P), blk_i[:, k, :]).then_inc(s_blk, 16)
            sp.wait_ge(s_blk, 32)
            sp.dma_start(blkrow[:, :, :], blkfile.unsqueeze(0)).then_inc(s_blk, 16)
            sp.wait_ge(s_x0, 1)
            sp.dma_start(x_sb[:, 0:NBLK - 1, :], node_rows(x[0:(NBLK - 1) * P, :])).then_inc(s_xin, 16)
            sp.dma_start(x_sb[0:REST, NBLK - 1, :], x[(NBLK - 1) * P:N, :]).then_inc(s_xin, 16)

            for l, kind in enumerate(PASSES):
                sp.wait_ge(s_y, l + 1)
                tv = node_rows(table[l])
                if l == 0:
                    half = NBLK // 2
                    sp.dma_start(tv[:, 0:half, :], hs[:, 0:half, :]).then_inc(s_tab, 16)
                    sp.dma_start(tv[:, half:NBLK, :], hs[:, half:NBLK, :]).then_inc(s_tab, 16)
                elif l == LAST:
                    sp.dma_start(tv[:, :, 0:F], tmp).then_inc(s_tab, 16)
                    sp.dma_start(tv[:, :, F:2 * F], h_sb).then_inc(s_tab, 16)
                else:
                    sp.dma_start(tv[:, :, 0:F // 2], tmp[:, :, 0:F // 2]).then_inc(s_tab, 16)
                    sp.dma_start(tv[:, :, F // 2:F], tmp[:, :, F // 2:F]).then_inc(s_tab, 16)

                def load_parts(i):
                    for q in range(NPART):
                        if l > 0 or not isfirst(i):
                            sp.wait_ge(s_freed[q], i + l * ITERS)
                        g = i * (NPART * PG) + q * PG
                        if kind == "B":
                            sp.dma_start(recB[:, q, :, :].rearrange("p (g j) c -> p g (j c)", j=JT),
                                         fileB_v[:, bass.ds(g, PG), :, :].rearrange("p g j c -> p g (j c)")).then_inc(s_rec[q], 16)
                        elif l == LAST:
                            sp.dma_start(rec[:, q, :, :].rearrange("p (g j) c -> p g (j c)", j=JT),
                                         fileA_v[:, bass.ds(g, PG), :, :].rearrange("p g j c -> p g (j c)")).then_inc(s_rec[q], 16)
                        else:
                            for j in range(JT):
                                sp.dma_start(rec[:, q, :, F:RA].rearrange("p (g j) c -> p g j c", j=JT)[:, :, j, :],
                                             fileA_v[:, bass.ds(g, PG), j, F:RA]).then_inc(s_rec[q], 16)

                turns(sp, ITERS, load_parts, first=int(l == 0))
            sp.wait_ge(s_y, LAST + 2)
            sp.dma_start(node_rows(out[0:(NBLK - 1) * P, :]), x_sb[:, 0:NBLK - 1, :]).then_inc(s_out, 16)
            sp.dma_start(out[(NBLK - 1) * P:N, :], x_sb[0:REST, NBLK - 1, :]).then_inc(s_out, 16)
            sp.wait_ge(s_out, 32)

        @block.gpsimd
        def _(pool):
            nc.gpsimd.iota(iota_i[:, :], [[1, P]], base=0, channel_multiplier=0).then_inc(s_iota, 1)
            nc.gpsimd.iota(part_i[:, :], [[0, 1]], base=0, channel_multiplier=1).then_inc(s_iota, 1)
            nc.gpsimd.iota(gnum_i[:, :], [[1, NG // P]], base=0, channel_multiplier=NG // P).then_inc(s_iota, 1)
            pool.wait_ge(s_fill, 2 * 16 * (SLOTS // (P * FILL)))
            with pool.Fori(0, TURNS) as i:
                for c in range(CHUNKS):
                    pool.wait_ge(s_wld[c], i * 16 + 16)
                    pool.wait_ge(s_rows[c], i + 1)
                    pool.wait_ge(s_pos[c], i + 1)
                    pool.sem_inc(s_go, 1)
                    for t in range(SC):
                        pool.indirect_dma_start(fileA, bass.IndirectOffsetOnAxis(ap=posI[:, c, t, 0:1], axis=0),
                                                rowA[:, c, t, :], None).then_inc(s_sc[c], 16)
                        pool.indirect_dma_start(fileB, bass.IndirectOffsetOnAxis(ap=posI[:, c, t, 1:2], axis=0),
                                                rowB[:, c, t, :], None).then_inc(s_sc[c], 16)
            for l, kind in enumerate(PASSES):
                index = recB[:, :, :, 1:2] if kind == "B" else rec[:, :, :, A_IDX:A_IDX + 1]
                pool.wait_ge(s_tab, 32 * (l + 1))
                with pool.Fori(0, ITERS) as i:
                    for q in range(NPART):
                        pool.wait_ge(s_rec[q], i * LOADS[l] + (LOADED[l] + LOADS[l]))
                        pool.sem_inc(s_go, 1)
                        for t in range(PT):
                            pool.indirect_dma_start(gat[:, q, t, 0:TABW[l]], None, table[l], bass.IndirectOffsetOnAxis(
                                ap=index[:, q, t, :].bitcast(I32), axis=0)).then_inc(s_gat[l // 3][q], 16)

        @block.tensor
        def _(pe):
            cnt = [bank[0], bank[1]]
            rank = bank[2]
            deg = [bank[3], bank[4]]
            pe.wait_ge(s_const, 1)
            for k in range(2):
                nc.tensor.matmul(cnt[k][:, 0:SC * NBLK], ones_b[:, :], zeros_b[:, 0:SC * NBLK],
                                 start=True, stop=False, skip_group_check=True)
            with pe.Fori(0, TURNS) as i:
                for c in range(CHUNKS):
                    pe.wait_ge(s_ckey[c], i + 1)
                    for k in range(2):
                        mm = nc.tensor.matmul(cnt[k][:, 0:SC * NBLK], ones_b[:, :], ohkey[:, c, :, k, :],
                                              start=False, stop=False, skip_group_check=True)
                    mm.then_inc(s_cnt[c], 1)
            pe.wait_ge(s_start, 1)
            nc.tensor.matmul(rank[:, 0:2 * NBLK], ident[:, :], start_rows, start=True, stop=False, skip_group_check=True)
            for k in range(2):
                nc.tensor.matmul(deg[k][:, 0:NBLK], ones_b[:, :], zeros_b[:, 0:NBLK],
                                 start=True, stop=False, skip_group_check=True)
            with pe.Fori(0, TURNS) as i:
                for c in range(CHUNKS):
                    pe.wait_ge(s_skey[c], i + 1)
                    for t in range(SC):
                        nc.tensor.matmul(rank[:, 0:2 * NBLK], before[:, :], ohkey[:, c, t, :, :].rearrange("p k b -> p (k b)"),
                                         start=False, stop=False, skip_group_check=True).then_inc(s_rank, 1)
                        for k in range(2):
                            nc.tensor.matmul(deg[k][:, 0:NBLK], ohlo[:, c, t, k, :], ohkey[:, c, t, k, :],
                                             start=False, stop=False, skip_group_check=True)
                        pe.wait_ge(s_read, i * (CHUNKS * SC) + (c * SC + t + 1))
                        mm = nc.tensor.matmul(rank[:, 0:2 * NBLK], upto[:, :], ohkey[:, c, t, :, :].rearrange("p k b -> p (k b)"),
                                              start=False, stop=False, skip_group_check=True)
                    mm.then_inc(s_chunk[c], 1)

            def sums(l, i, q, left, right):
                n = i * NPART + (l * NPP + q)
                for t in range(PT):
                    k = t // JT
                    mm = nc.tensor.matmul(bank[4 + q % 2][:, k * F:k * F + F], left[:, t, :], right[:, t, 0:F],
                                          start=(t % JT == 0), stop=(t % JT == JT - 1))
                mm.then_inc(s_agg, 1)

            def attend_back(i, q):
                pe.wait_ge(s_p, i * NPART + q + 1)
                for t in range(PT):
                    mm = nc.tensor.transpose(bank[2 + t // 4][:, t % 4 * P:t % 4 * P + P], sc[:, t * P:t * P + P], ident[:, :])
                mm.then_inc(s_pt, 1)
                pe.wait_ge(s_ptc, i * NPART + q + 1)
                sums(0, i, q, probs, gat[:, q, :, :])

            def attend(i):
                for q in range(NPART):
                    if q > 0:
                        attend_back(i, q - 1)
                    elif not isfirst(i):
                        attend_back(i - 1, NPART - 1)
                    pe.wait_ge(s_msk, i * NPART + q + 1)
                    for t in range(PT):
                        mm = nc.tensor.transpose(bank[t // 4][:, t % 4 * P:t % 4 * P + P], ohT[:, t, :], ident[:, :])
                    mm.then_inc(s_zt, 1)

            turns(pe, ITERS, attend)
            attend_back(ITERS - 1, NPART - 1)
            for l in range(1, LAST):
                with pe.Fori(0, ITERS) as i:
                    for q in range(NPART):
                        pe.wait_ge(s_oh, i * NPART + (l * NPP + q + 1))
                        pe.wait_ge(s_gat[l // 3][q], i * (16 * PT) + (l % 3 * ITERS + 1) * 16 * PT)
                        sums(l, i, q, oh[:, q % 2, :, :], gat[:, q, :, :])

            def project(weights, width, n0):
                def pair(i):
                    pe.wait_ge(s_two, i + (n0 + 1))
                    nc.tensor.transpose(bank[0][:, 0:P], two[:, :], ident[:, :]).then_inc(s_tr, 1)
                    pe.wait_ge(s_trc, i + (n0 + 1))
                    if n0 > 0 or not isfirst(i):
                        pe.wait_ge(s_prc, i + n0)
                    nc.tensor.matmul(bank[1][:, 0:width], hT[:, :], weights, start=True, stop=True).then_inc(s_pr, 1)

                turns(pe, NBLK // 2, pair)

            pe.wait_ge(s_win, 24 * 16)
            project(Wqk[:, :, :, :].rearrange("p b k f -> p (b k f)"), 4 * F, 0)
            pe.wait_ge(s_prc, NBLK // 2)
            breg = [pe.alloc_register(f"block{k}") for k in range(PG)]

            def edge_queries(i, q):
                n = i * NPART + q
                pe.load(breg, blkrow[0:1, 0, bass.ds(i * (NPART * PG) + q * PG, PG)])
                blocks = [pe.snap(r, min_val=0, max_val=NBLK - 1) for r in breg]
                pe.wait_ge(s_oh, n + (LAST * NPP + 1))
                for t in range(PT):
                    mm = nc.tensor.transpose(bank[t // 4][:, t % 4 * P:t % 4 * P + P], oh[:, q % 2, t, :], ident[:, :])
                mm.then_inc(s_oT, 1)
                pe.wait_ge(s_oTc, n + 1)
                for t in range(PT):
                    mm = nc.tensor.matmul(bank[2][:, t * F:t * F + F], ohT[:, t, :],
                                          q_sb[:, bass.ds(blocks[t // JT], 1), :].rearrange("p b f -> p (b f)"),
                                          start=True, stop=True)
                mm.then_inc(s_qg, 1)

            def pairs(i):
                for q in range(NPART):
                    pe.wait_ge(s_msg, i * NPART + q + 1)
                    sums(LAST, i, q, oh[:, q % 2, :, :], msg)
                    if q < NPART - 1:
                        edge_queries(i, q + 1)
                    elif not islast(i):
                        edge_queries(i + 1, 0)

            edge_queries(0, 0)
            turns(pe, ITERS, pairs, first=0, last=1)
            project(Wvb[:, :, :].rearrange("p b f -> p (b f)"), 2 * F, NBLK // 2)

        @block.scalar
        def _(act):
            act.wait_ge(s_const, 1)
            def put_together(i):
                for c in range(CHUNKS):
                    if not isfirst(i):
                        act.wait_ge(s_sc[c], i * (2 * SC * 16))
                    cols = bass.ds(i * (SC * CHUNKS) + c * SC, SC)
                    nc.scalar.copy(rowA[:, c, :, A_LO], los[:, 2, cols])
                    nc.scalar.copy(rowA[:, c, :, A_LON], los[:, 0, cols])
                    nc.scalar.copy(rowA[:, c, :, A_PHI], phi[:, cols])
                    nc.scalar.copy(rowA[:, c, :, A_IDX].bitcast(I32), dstI[:, cols])
                    nc.scalar.copy(rowB[:, c, :, 0], los[:, 1, cols])
                    nc.scalar.copy(rowB[:, c, :, 1].bitcast(I32), srcI[:, cols]).then_inc(s_rows[c], 1)

            turns(act, TURNS, put_together)

            def root(n, rows):
                act.wait_ge(s_var, n)
                nc.scalar.activation(stat[:, rows, :], stat[:, rows, :], ACT.Sqrt).then_inc(s_root, 1)

            root(1, slice(0, 2))
            root(2, slice(1, 2))
            def exponentials(i, q):
                n = i * NPART + q
                act.wait_ge(s_l, n + 1)
                nc.scalar.activation(fac[:, :], fall[:, :], ACT.Exp)
                for k in range(PG):
                    g = slice(k * GROUP, k * GROUP + GROUP)
                    a = nc.scalar.activation(sc[:, g], sc[:, g], ACT.Exp, bias=lowest[:, k:k + 1],
                                             accum_out=rsum[:, k:k + 1])
                a.then_inc(s_p, 1)

            def attend(i):
                for q in range(NPART):
                    n = i * NPART + q
                    if q > 0:
                        exponentials(i, q - 1)
                    elif not isfirst(i):
                        exponentials(i - 1, NPART - 1)
                    act.wait_ge(s_oh, n + 1)
                    if not (isfirst(i) and q == 0):
                        act.wait_ge(s_zt, n)
                    act.wait_ge(s_gat[0][q], i * (16 * PT) + 16 * PT)
                    for t in range(PT):
                        a = nc.scalar.activation(ohT[:, t, :], mask[:, t, :], ACT.Identity,
                                                 bias=gat[:, q, t, F:F + 1], scale=-HUGE)
                    a.then_inc(s_msk, 1)
                    act.wait_ge(s_zt, n + 1)
                    act.wait_ge(s_sic, n + 1)
                    if not (isfirst(i) and q == 0):
                        act.wait_ge(s_pt, n)
                    for k in range(PG):
                        a = nc.scalar.activation(sc[:, k * GROUP:k * GROUP + GROUP],
                                                 bank[k // 2][:, k % 2 * GROUP:k % 2 * GROUP + GROUP],
                                                 ACT.Identity, bias=sic[:, k:k + 1])
                    a.then_inc(s_t, 1)

            turns(act, ITERS, attend)
            exponentials(ITERS - 1, NPART - 1)

            def project(source, n0):
                def pair(i):
                    nc.scalar.copy(two[:, :].rearrange("p (b f) -> p b f", b=2),
                                   source[:, bass.ds(i * 2, 2), :]).then_inc(s_two, 1)
                    act.wait_ge(s_tr, i + (n0 + 1))
                    if n0 > 0 or not isfirst(i):
                        act.wait_ge(s_pr, i + n0)
                    nc.scalar.copy(hT[:, :], bank[0][:, 0:P]).then_inc(s_trc, 1)

                turns(act, NBLK // 2, pair)

            root(3, slice(1, 2))
            root(4, slice(1, 2))
            root(5, slice(1, 2))
            act.wait_ge(s_m, 1)
            project(h_sb, 0)

            def ones_out(i):
                for q in range(NPART):
                    n = i * NPART + q
                    act.wait_ge(s_oT, n + 1)
                    if not (isfirst(i) and q == 0):
                        act.wait_ge(s_qg, n)
                    for b in range(2):
                        a = nc.scalar.copy(ohT[:, 4 * b:4 * b + 4, :].rearrange("p t n -> p (t n)"), bank[b][:, :])
                    a.then_inc(s_oTc, 1)

            turns(act, ITERS, ones_out)
            act.wait_ge(s_accd, 1)
            project(acc, NBLK // 2)

        @block.vector
        def _(v):
            done = [0]

            def nth():
                done[0] += 1
                return done[0]

            v.wait_ge(s_iota, 3)
            nc.vector.tensor_copy(iota[:, :], iota_i[:, :]).then_inc(s_dve, 1)
            v.wait_ge(s_dve, nth())
            nc.vector.tensor_copy(part[:, :], part_i[:, :]).then_inc(s_dve, 1)
            v.wait_ge(s_dve, nth())
            nc.vector.tensor_copy(gnum[:, :], gnum_i[:, :])
            nc.vector.tensor_copy(iota_b[:, :], iota_i[:, :])
            nc.vector.tensor_scalar(ident[:, :], iota[:, :], part[:, 0:1], None, ALU.is_equal)
            nc.vector.tensor_scalar(before[:, :], iota[:, :], part[:, 0:1], None, ALU.is_gt)
            nc.vector.tensor_scalar(upto[:, :], iota[:, :], part[:, 0:1], None, ALU.is_le)
            nc.vector.memset(ones_b[:, :], 1.0)
            nc.vector.memset(zeros_b[:, :], 0.0)
            nc.vector.memset(Wqk[:, :, :, :], 0.0)
            nc.vector.memset(Wvb[:, :, :], 0.0).then_inc(s_w0, 1)
            nc.vector.memset(fillA[:, :, :], 0.0)
            nc.vector.memset(fillB[:, :, :], 0.0).then_inc(s_dve, 1)
            v.wait_ge(s_dve, nth())
            nc.vector.memset(fillA[:, :, A_LO:A_LON + 1], -1.0)
            nc.vector.memset(fillB[:, :, 0:1], -1.0).then_inc(s_fillsrc, 1)
            v.wait_ge(s_in, 6 * 16)
            for k, ends in enumerate((srcI, dstI)):
                nc.vector.tensor_single_scalar(work_i, ends, 7, ALU.arith_shift_right).then_inc(s_dve, 1)
                v.wait_ge(s_dve, nth())
                nc.vector.tensor_copy(keys[:, k, 0:T], work_i).then_inc(s_dve, 1)
                v.wait_ge(s_dve, nth())
                nc.vector.tensor_single_scalar(work_i, ends, P - 1, ALU.bitwise_and).then_inc(s_dve, 1)
                v.wait_ge(s_dve, nth())
                nc.vector.tensor_copy(los[:, 2 - k, 0:T], work_i).then_inc(s_dve, 1)
                v.wait_ge(s_dve, nth())
            nc.vector.tensor_tensor(phi, phi, phi2, ALU.mult)
            nc.vector.tensor_tensor(work_i.bitcast(F32), srcI, dstI, ALU.not_equal)
            nc.vector.tensor_scalar(los[:, 0, 0:T], los[:, 2, 0:T], 1.0, None, ALU.add).then_inc(s_dve, 1)
            v.wait_ge(s_dve, nth())
            nc.vector.tensor_tensor(los[:, 0, 0:T], los[:, 0, 0:T], work_i.bitcast(F32), ALU.mult).then_inc(s_dve, 1)
            v.wait_ge(s_dve, nth())
            nc.vector.tensor_scalar(los[:, 0, 0:T], los[:, 0, 0:T], -1.0, None, ALU.add).then_inc(s_const, 1)
            v.wait_ge(s_const, 1)

            def ones_by_block(c, i):
                cols = bass.ds(i * (SC * CHUNKS) + c * SC, SC)
                for k in range(2):
                    last = nc.vector.tensor_tensor(
                        ohkey[:, c, :, k, :], iota_b[:, 0:NBLK].unsqueeze(1).broadcast_to((P, SC, NBLK)),
                        keys[:, k, cols].unsqueeze(2).broadcast_to((P, SC, NBLK)), ALU.is_equal)
                return last

            def count(i):
                for c in range(CHUNKS):
                    if not isfirst(i):
                        v.wait_ge(s_cnt[c], i)
                    ones_by_block(c, i).then_inc(s_ckey[c], 1)

            turns(v, TURNS, count)
            for c in range(CHUNKS):
                v.wait_ge(s_cnt[c], TURNS)
            for k in range(2):
                nc.vector.tensor_reduce(cntf[:, k, :], bank[k][:, 0:SC * NBLK].rearrange("p (t b) -> p b t", t=SC),
                                        AX.X, ALU.add).then_inc(s_dve, 1)
                v.wait_ge(s_dve, nth())
            nc.vector.tensor_scalar(cnti[:, :, :], cntf[:, :, :], float(GROUP - 1), None, ALU.add).then_inc(s_dve, 1)
            v.wait_ge(s_dve, nth())
            nc.vector.tensor_single_scalar(cnti[:, :, :], cnti[:, :, :], GROUP.bit_length() - 1,
                                           ALU.arith_shift_right).then_inc(s_dve, 1)
            v.wait_ge(s_dve, nth())
            nc.vector.tensor_copy(cntf[:, :, :], cnti[:, :, :]).then_inc(s_dve, 1)
            v.wait_ge(s_dve, nth())
            for k in range(2):
                nc.vector.tensor_tensor_scan(start[:, k, :], cntf[:, k, :], zeros_b[:, 0:NBLK], 0.0, ALU.add, ALU.add).then_inc(s_dve, 1)
                v.wait_ge(s_dve, nth())
            nc.vector.tensor_tensor(start[:, :, :], start[:, :, :], cntf[:, :, :], ALU.subtract).then_inc(s_dve, 1)
            v.wait_ge(s_dve, nth())
            nc.vector.tensor_scalar(start_rows, start[:, :, :].rearrange("p k b -> p (k b)"), float(GROUP), None,
                                    ALU.mult).then_inc(s_start, 1)
            GC = NG // P
            for k in range(2):
                cmp = oh_area[:, 0:GC * NBLK].rearrange("p (g b) -> p g b", b=NBLK)
                nc.vector.tensor_tensor(cmp, start[:, k, :].unsqueeze(1).broadcast_to((P, GC, NBLK)),
                                        gnum[:, :].unsqueeze(2).broadcast_to((P, GC, NBLK)), ALU.is_le).then_inc(s_dve, 1)
                v.wait_ge(s_dve, nth())
                nc.vector.tensor_reduce(trash[:, 0, 0:GC], cmp, AX.X, ALU.add).then_inc(s_dve, 1)
                v.wait_ge(s_dve, nth())
                nc.vector.tensor_scalar(blk_i[:, k, :], trash[:, 0, 0:GC], -1.0, None, ALU.add).then_inc(s_dve, 1)
                v.wait_ge(s_dve, nth())
            v.sem_inc(s_blki, 1)

            def sort(i):
                for c in range(CHUNKS):
                    if not isfirst(i):
                        v.wait_ge(s_chunk[c], i)
                    ones_by_block(c, i)
                    cols = bass.ds(i * (SC * CHUNKS) + c * SC, SC)
                    for k in range(2):
                        last = nc.vector.tensor_tensor(
                            ohlo[:, c, :, k, :], iota_b[:, :].unsqueeze(1).broadcast_to((P, SC, P)),
                            los[:, k, cols].unsqueeze(2).broadcast_to((P, SC, P)), ALU.is_equal)
                    last.then_inc(s_skey[c], 1)
                    v.wait_ge(s_skey[c], i + 1)
                    for t in range(SC):
                        v.wait_ge(s_rank, i * (CHUNKS * SC) + (c * SC + t + 1))
                        for k in range(2):
                            last = nc.vector.tensor_tensor_reduce(
                                trash[:, k, :], ohkey[:, c, t, k, :], bank[2][:, k * NBLK:k * NBLK + NBLK],
                                1.0, 0.0, ALU.mult, ALU.add, pos[:, c, t, k:k + 1])
                        last.then_inc(s_read, 1)
                    v.wait_ge(s_read, i * (CHUNKS * SC) + (c * SC + SC))
                    if not isfirst(i):
                        v.wait_ge(s_sc[c], i * (2 * SC * 16))
                    nc.vector.tensor_copy(posI[:, c, :, :], pos[:, c, :, :]).then_inc(s_pos[c], 1)

            turns(v, TURNS, sort)
            for c in range(CHUNKS):
                v.wait_ge(s_chunk[c], TURNS)
            for k in range(2):
                nc.vector.tensor_copy(degs[:, k, :], bank[3 + k][:, 0:NBLK]).then_inc(s_dve, 1)
                v.wait_ge(s_dve, nth())
            nc.vector.tensor_scalar(stat[:, 0, :], degs[:, 0, :], 1.0, None, ALU.add)
            nc.vector.tensor_scalar(stat[:, 1, :], degs[:, 1, :], 1.0, None, ALU.max).then_inc(s_var, 1)
            v.wait_ge(s_root, 1)
            nc.vector.reciprocal(dinv1[:, :], stat[:, 0, :]).then_inc(s_dve, 1)
            v.wait_ge(s_dve, nth())
            nc.vector.reciprocal(dinv2[:, :], stat[:, 1, :]).then_inc(s_dve, 1)
            v.wait_ge(s_dve, nth())
            nc.vector.tensor_scalar(trash[:, 0, :], degs[:, 1, :], 0.0, None, ALU.is_gt).then_inc(s_dve, 1)
            v.wait_ge(s_dve, nth())
            nc.vector.tensor_tensor(dinv2[:, :], dinv2[:, :], trash[:, 0, :], ALU.mult).then_inc(s_dve, 1)
            v.wait_ge(s_dve, nth())
            for c in range(CHUNKS):
                v.wait_ge(s_sc[c], TURNS * 2 * SC * 16)
            nc.vector.memset(x_sb[:, NBLK - 1, :], 0.0).then_inc(s_x0, 1)
            v.wait_ge(s_xin, 32)

            def by_node(col):
                return col.unsqueeze(2).broadcast_to((P, NBLK, F))

            roots = [1]

            def layernorm():
                nc.vector.tensor_reduce(stat[:, 0, :], x_sb, AX.X, ALU.add).then_inc(s_dve, 1)
                v.wait_ge(s_dve, nth())
                nc.vector.tensor_scalar(stat[:, 0, :], stat[:, 0, :], -1.0 / F, None, ALU.mult).then_inc(s_dve, 1)
                v.wait_ge(s_dve, nth())
                nc.vector.tensor_tensor(tmp, x_sb, by_node(stat[:, 0, :]), ALU.add).then_inc(s_dve, 1)
                v.wait_ge(s_dve, nth())
                nc.vector.tensor_tensor(h_sb, tmp, tmp, ALU.mult).then_inc(s_dve, 1)
                v.wait_ge(s_dve, nth())
                nc.vector.tensor_reduce(stat[:, 1, :], h_sb, AX.X, ALU.add).then_inc(s_dve, 1)
                v.wait_ge(s_dve, nth())
                nc.vector.tensor_scalar(stat[:, 1, :], stat[:, 1, :], 1.0 / F, EPS, ALU.mult, ALU.add).then_inc(s_var, 1)
                roots[0] += 1
                v.wait_ge(s_root, roots[0])
                nc.vector.reciprocal(stat[:, 1, :], stat[:, 1, :]).then_inc(s_dve, 1)
                v.wait_ge(s_dve, nth())
                nc.vector.tensor_tensor(h_sb, tmp, by_node(stat[:, 1, :]), ALU.mult).then_inc(s_dve, 1)
                v.wait_ge(s_dve, nth())
                nc.vector.tensor_scalar(h_sb, h_sb, 0.0, None, ALU.max).then_inc(s_dve, 1)
                v.wait_ge(s_dve, nth())

            breg = [v.alloc_register(f"vblock{k}") for k in range(PG)]

            def load_blocks(kind, i, q):
                which = 0 if kind == "A" else 1
                v.load(breg, blkrow[0:1, which, bass.ds(i * (NPART * PG) + q * PG, PG)])
                return [v.snap(r, min_val=0, max_val=NBLK - 1) for r in breg]

            def ones_by_node(names, op, q):
                nc.vector.tensor_tensor(oh[:, q % 2, :, :], iota[:, :].unsqueeze(1).broadcast_to((P, PT, P)),
                                        names.unsqueeze(2).broadcast_to((P, PT, P)), op).then_inc(s_oh, 1)

            v.wait_ge(s_blk, 48)
            layernorm()
            for k in range(2):
                nc.vector.tensor_tensor(tmp, h_sb, wcols[:, k, :].unsqueeze(1).broadcast_to((P, NBLK, F)), ALU.mult).then_inc(s_dve, 1)
                v.wait_ge(s_dve, nth())
                nc.vector.tensor_reduce(stat[:, k, :], tmp, AX.X, ALU.add).then_inc(s_dve, 1)
                v.wait_ge(s_dve, nth())
            nc.vector.tensor_tensor(trash[:, 0, :], stat[:, 0, :], stat[:, 1, :], ALU.add).then_inc(s_dve, 1)
            v.wait_ge(s_dve, nth())
            nc.vector.scalar_tensor_tensor(trash[:, 1, :], trash[:, 0, :], 0.01, trash[:, 0, :], ALU.mult, ALU.max).then_inc(s_dve, 1)
            v.wait_ge(s_dve, nth())
            nc.vector.tensor_scalar(stat[:, 2, :], trash[:, 1, :], -1.0, None, ALU.mult)
            nc.vector.memset(stat[:, 3, :], 1.0)
            nc.vector.tensor_copy(hs[:, :, 0:F], h_sb)
            nc.vector.tensor_copy(hs[:, :, F], stat[:, 1, :])
            nc.vector.tensor_copy(acc, h_sb).then_inc(s_dve, 1)
            v.wait_ge(s_dve, nth())
            v.sem_inc(s_y, 1)

            def masks(i, q):
                n = i * NPART + q
                v.wait_ge(s_rec[q], i * 16 + 16)
                if not (isinstance(n, int) and n == 0):
                    v.wait_ge(s_msk, n)
                nc.vector.tensor_tensor(mask, iota[:, :].unsqueeze(1).broadcast_to((P, PT, P)),
                                        recB[:, q, :, 0].unsqueeze(2).broadcast_to((P, PT, P)), ALU.not_equal).then_inc(s_oh, 1)

            def weighted_sums(i, q):
                n = i * NPART + q
                v.wait_ge(s_pt, n + 1)
                for r in range(2):
                    a = nc.vector.tensor_copy(probs[:, 4 * r:4 * r + 4, :].rearrange("p t n -> p (t n)"), bank[2 + r][:, :])
                a.then_inc(s_ptc, 1)
                b = load_blocks("B", i, q)
                v.wait_ge(s_agg, n + 1)
                for k in range(PG):
                    here = acc[:, bass.ds(b[k], 1), :].rearrange("p b f -> p (b f)")
                    den = stat[:, 3, bass.ds(b[k], 1)]
                    nc.vector.scalar_tensor_tensor(den, den, fac[:, k:k + 1], rsum[:, k:k + 1], ALU.mult, ALU.add)
                    nc.vector.scalar_tensor_tensor(here, here, fac[:, k:k + 1], bank[4 + q % 2][:, k * F:k * F + F],
                                                   ALU.mult, ALU.add).then_inc(s_acc, 1)
                    v.wait_ge(s_acc, n * PG + (k + 1))
                v.sem_inc(s_freed[q], 1)

            def attend(i):
                STEPS = 2 + 3 * PG
                for q in range(NPART):
                    n = i * NPART + q
                    if q > 0:
                        weighted_sums(i, q - 1)
                    elif not isfirst(i):
                        weighted_sums(i - 1, NPART - 1)
                    b = load_blocks("B", i, q)
                    for k in range(PG):
                        a = nc.vector.tensor_copy(sic[:, k:k + 1], stat[:, 0, bass.ds(b[k], 1)])
                    a.then_inc(s_sic, 1)
                    if q < NPART - 1:
                        masks(i, q + 1)
                    elif not islast(i):
                        masks(i + 1, 0)
                    v.wait_ge(s_t, n + 1)
                    nc.vector.scalar_tensor_tensor(sc[:, :], sc[:, :], 0.01, sc[:, :], ALU.mult, ALU.max).then_inc(s_low, 1)
                    v.wait_ge(s_low, n * STEPS + 1)
                    nc.vector.tensor_reduce(gmax[:, :], sc[:, :].rearrange("p (k e) -> p k e", k=PG), AX.X, ALU.max).then_inc(s_low, 1)
                    v.wait_ge(s_low, n * STEPS + 2)
                    for k in range(PG):
                        low = stat[:, 2, bass.ds(b[k], 1)]
                        nc.vector.scalar_tensor_tensor(lowest[:, k:k + 1], gmax[:, k:k + 1], -1.0, low, ALU.mult, ALU.min).then_inc(s_low, 1)
                        v.wait_ge(s_low, n * STEPS + (3 + 3 * k))
                        nc.vector.tensor_tensor(fall[:, k:k + 1], lowest[:, k:k + 1], low, ALU.subtract).then_inc(s_low, 1)
                        v.wait_ge(s_low, n * STEPS + (4 + 3 * k))
                        nc.vector.tensor_scalar(low, lowest[:, k:k + 1], 1.0, None, ALU.mult).then_inc(s_low, 1)
                        v.wait_ge(s_low, n * STEPS + (5 + 3 * k))
                    v.sem_inc(s_l, 1)

            masks(0, 0)
            turns(v, ITERS, attend, last=1)
            weighted_sums(ITERS - 1, NPART - 1)
            nc.vector.reciprocal(stat[:, 3, :], stat[:, 3, :]).then_inc(s_dve, 1)
            v.wait_ge(s_dve, nth())
            nc.vector.tensor_tensor(acc, acc, by_node(stat[:, 3, :]), ALU.mult).then_inc(s_dve, 1)
            v.wait_ge(s_dve, nth())
            nc.vector.scalar_tensor_tensor(x_sb, acc, 0.0, x_sb, ALU.max, ALU.add).then_inc(s_dve, 1)
            v.wait_ge(s_dve, nth())

            def plain(l, names):
                with v.Fori(0, ITERS) as i:
                    for q in range(NPART):
                        n = i * NPART + (l * NPP + q)
                        b = load_blocks(PASSES[l], i, q)
                        v.wait_ge(s_rec[q], i * LOADS[l] + (LOADED[l] + LOADS[l]))
                        ones_by_node(names[:, q, :], ALU.is_equal, q)
                        v.wait_ge(s_agg, n + 1)
                        add_sums(l, n, q, b)

            def add_sums(l, n, q, b):
                for k in range(PG):
                    here = acc[:, bass.ds(b[k], 1), :].rearrange("p b f -> p (b f)")
                    nc.vector.tensor_tensor(here, here, bank[4 + q % 2][:, k * F:k * F + F], ALU.add).then_inc(s_acc, 1)
                    v.wait_ge(s_acc, n * PG + (k + 1))
                v.sem_inc(s_freed[q], 1)

            layernorm()
            nc.vector.tensor_tensor(tmp, h_sb, by_node(dinv1[:, :]), ALU.mult).then_inc(s_dve, 1)
            v.wait_ge(s_dve, nth())
            nc.vector.tensor_copy(acc, tmp).then_inc(s_dve, 1)
            v.wait_ge(s_dve, nth())
            v.sem_inc(s_y, 1)
            plain(1, rec[:, :, :, A_LON])
            nc.vector.tensor_tensor(acc, acc, by_node(dinv1[:, :]), ALU.mult).then_inc(s_dve, 1)
            v.wait_ge(s_dve, nth())
            nc.vector.tensor_tensor(x_sb, x_sb, acc, ALU.add).then_inc(s_dve, 1)
            v.wait_ge(s_dve, nth())

            layernorm()
            nc.vector.tensor_copy(q_sb, h_sb)
            nc.vector.tensor_tensor(tmp, h_sb, by_node(dinv2[:, :]), ALU.mult).then_inc(s_dve, 1)
            v.wait_ge(s_dve, nth())
            for l in range(2, LAST):
                nc.vector.memset(acc, 0.0).then_inc(s_dve, 1)
                v.wait_ge(s_dve, nth())
                v.sem_inc(s_y, 1)
                plain(l, recB[:, :, :, 0])
                nc.vector.tensor_tensor(acc, acc, by_node(dinv2[:, :]), ALU.mult).then_inc(s_dve, 1)
                v.wait_ge(s_dve, nth())
                nc.vector.tensor_tensor(q_sb, q_sb, acc, ALU.add).then_inc(s_dve, 1)
                v.wait_ge(s_dve, nth())
                nc.vector.tensor_tensor(tmp, acc, by_node(dinv2[:, :]), ALU.mult).then_inc(s_dve, 1)
                v.wait_ge(s_dve, nth())
            nc.vector.scalar_tensor_tensor(x_sb, q_sb, 0.25, x_sb, ALU.mult, ALU.add).then_inc(s_dve, 1)
            v.wait_ge(s_dve, nth())

            layernorm()
            nc.vector.memset(acc, 0.0).then_inc(s_dve, 1)
            v.wait_ge(s_dve, nth())
            v.sem_inc(s_m, 1)
            with v.Fori(0, NBLK // 2) as i:
                v.wait_ge(s_pr, i + 1)
                both = bank[1][:, 0:4 * F].rearrange("p (b k f) -> p b k f", b=2, k=2)
                nc.vector.tensor_copy(q_sb[:, bass.ds(i * 2, 2), :], both[:, :, 0, :])
                nc.vector.tensor_copy(tmp[:, bass.ds(i * 2, 2), :], both[:, :, 1, :]).then_inc(s_prc, 1)
            v.wait_ge(s_prc, NBLK // 2)
            v.sem_inc(s_y, 1)
            SCALE = float(D) ** -0.5

            def pair_ones(i, q):
                v.wait_ge(s_rec[q], i * 16 + (LOADED[LAST] + 16))
                ones_by_node(rec[:, q, :, A_LO], ALU.is_equal, q)

            def pairs(i):
                STEPS = 4
                for q in range(NPART):
                    n = i * NPART + q
                    v.wait_ge(s_gat[LAST // 3][q], i * (16 * PT) + (LAST % 3 * ITERS + 1) * 16 * PT)
                    nc.vector.tensor_tensor(msg2, rec[:, q, :, 0:F], gat[:, q, :, 0:F], ALU.mult).then_inc(s_m, 1)
                    v.wait_ge(s_m, n * STEPS + 2)
                    v.wait_ge(s_qg, n + 1)
                    nc.vector.tensor_tensor(msg2, msg2, bank[2][:, 0:PT * F].rearrange("p (t f) -> p t f", t=PT), ALU.mult).then_inc(s_m, 1)
                    v.wait_ge(s_m, n * STEPS + 3)
                    nc.vector.tensor_reduce(alpha[:, :, :], msg2.rearrange("p t (h d) -> p t h d", h=HEADS), AX.X, ALU.add).then_inc(s_m, 1)
                    v.wait_ge(s_m, n * STEPS + 4)
                    nc.vector.scalar_tensor_tensor(alpha[:, :, :], alpha[:, :, :], SCALE,
                                                   rec[:, q, :, A_PHI].unsqueeze(2).broadcast_to((P, PT, HEADS)),
                                                   ALU.mult, ALU.mult).then_inc(s_m, 1)
                    v.wait_ge(s_m, n * STEPS + 5)
                    nc.vector.tensor_tensor(msg.rearrange("p t (h d) -> p t h d", h=HEADS),
                                            gat[:, q, :, F:2 * F].rearrange("p t (h d) -> p t h d", h=HEADS),
                                            alpha[:, :, :].unsqueeze(3).broadcast_to((P, PT, HEADS, D)), ALU.mult).then_inc(s_msg, 1)
                    if q < NPART - 1:
                        pair_ones(i, q + 1)
                    elif not islast(i):
                        pair_ones(i + 1, 0)
                    b = load_blocks("A", i, q)
                    v.wait_ge(s_agg, n + (LAST * NPP + 1))
                    add_sums(LAST, i * NPART + (LAST * NPP + q), q, b)

            pair_ones(0, 0)
            turns(v, ITERS, pairs, first=0, last=1)
            v.sem_inc(s_accd, 1)
            with v.Fori(0, NBLK // 2) as i:
                v.wait_ge(s_pr, i + (NBLK // 2 + 1))
                xs = x_sb[:, bass.ds(i * 2, 2), :]
                nc.vector.tensor_tensor(xs, xs, bank[1][:, 0:2 * F].rearrange("p (b f) -> p b f", b=2), ALU.add).then_inc(s_prc, 1)
            v.wait_ge(s_prc, NBLK)
            v.sem_inc(s_y, 1)


_INS = ["x", "src", "dst", "edge_attr_64", "edge_weight", "edge_weight_n2",
        "L0_gnn_w_i", "L0_gnn_w_j", "L3_gnn_Wq", "L3_gnn_Wk", "L3_gnn_Wv"]


def kernel(**inputs):
    import numpy as np
    import concourse.bacc as bacc
    from concourse import mybir as mb
    from concourse.bass_utils import run_bass_kernel_spmd

    nc = bacc.Bacc("TRN2", target_bir_lowering=False, num_devices=1)
    arrays, args = {}, []
    for name in _INS:
        a = np.ascontiguousarray(inputs[name])
        arrays[f"in_{name}"] = a
        args.append(nc.dram_tensor(f"in_{name}", a.shape, mb.dt.from_np(a.dtype), kind="ExternalInput").ap())
    args.append(nc.dram_tensor("out_x", inputs["x"].shape, mb.dt.float32, kind="ExternalOutput").ap())
    gnn_four_layers(nc, *args)
    r = run_bass_kernel_spmd(nc, [arrays], core_ids=[0])
    return r.results[0]["out_x"]
```

```python
from contextlib import ExitStack

import concourse.bass as bass
from concourse import mybir

ALU = mybir.AluOpType
ACT = mybir.ActivationFunctionType
F32 = mybir.dt.float32
BF16 = mybir.dt.bfloat16
I32 = mybir.dt.int32
AX = mybir.AxisListType

P = 128
HUGE = 1.0e30


def gnn_four_layers(nc, x, src, dst, edge_attr, edge_weight, edge_weight2, w_i, w_j, Wq, Wk, Wv, out):
    N, F = x.shape
    E = src.shape[0]
    HEADS, D, _ = Wq.shape
    EPS = 1e-5
    NBLK = -(-N // P)
    REST = N - (NBLK - 1) * P
    ROWS = NBLK * P

    JT = 2
    GROUP = JT * P
    PT, PG = 8, 4
    NPART = 4
    most = E // GROUP + NBLK
    ITERS = -(-most // (NPART * PG))
    NG = ITERS * NPART * PG
    SLOTS = NG * GROUP
    RA = F + 4
    A_LO, A_LON, A_PHI, A_IDX = F, F + 1, F + 2, F + 3
    RB = 2

    T = E // P
    SC = 5
    CHUNKS = 5
    TURNS = T // (SC * CHUNKS)
    assert T * P == E and TURNS * SC * CHUNKS == T and D * HEADS == F

    fileA = nc.dram_tensor("fileA", (SLOTS, RA), F32, kind="Internal").ap()
    fileB = nc.dram_tensor("fileB", (SLOTS, RB), F32, kind="Internal").ap()
    blkfile = nc.dram_tensor("blkfile", (2, NG), I32, kind="Internal").ap()
    TABW = [F + 2, F, F, F, F, 2 * F]
    table = [nc.dram_tensor(f"table{l}", (ROWS, w), F32, kind="Internal").ap() for l, w in enumerate(TABW)]

    with ExitStack() as ctx:
        def sb(name, shape, dt=F32):
            return ctx.enter_context(nc.sbuf_tensor(name, shape, dt))

        def sem(name):
            return ctx.enter_context(nc.semaphore(name))

        iota_i = sb("iota_i", [P, P], I32)
        part_i = sb("part_i", [P, 1], I32)
        iota = sb("iota", [P, P])
        part = sb("part", [P, 1])
        iota_b = sb("iota_b", [P, P], BF16)
        ident = sb("ident", [P, P])
        before = sb("before", [P, P], BF16)
        upto = sb("upto", [P, P], BF16)
        ones_b = sb("ones_b", [P, P], BF16)
        blkrow = sb("blkrow", [1, 2, NG], I32)
        blk_i = sb("blk_i", [P, 2, NG // P], I32)
        wcols = sb("wcols", [P, 2, F])
        Wqk = sb("Wqk", [P, 2, 2, F])
        Wvb = sb("Wvb", [P, 2, F])
        degs = sb("degs", [P, 2, NBLK])
        dinv1 = sb("dinv1", [P, NBLK])
        dinv2 = sb("dinv2", [P, NBLK])
        stat = sb("stat", [P, 4, NBLK])
        start = sb("start", [P, 2, NBLK])
        start_r = sb("start_r", [P, 2, NBLK])
        start_rows = start_r[:, :, :].rearrange("p k b -> p (k b)")
        cntf = sb("cntf", [P, 2, NBLK])
        cnti = sb("cnti", [P, 2, NBLK], I32)
        gnum = sb("gnum", [P, NG // P])
        gnum_i = sb("gnum_i", [P, NG // P], I32)
        zeros_b = sb("zeros_b", [P, 512], BF16)

        BIG = NBLK * F
        area = sb("area", [P, 5 * BIG])
        x_sb = area[:, 0:BIG].rearrange("p (b f) -> p b f", f=F)
        h_sb = area[:, BIG:2 * BIG].rearrange("p (b f) -> p b f", f=F)
        acc = area[:, 2 * BIG:3 * BIG].rearrange("p (b f) -> p b f", f=F)
        tmp = area[:, 3 * BIG:4 * BIG].rearrange("p (b f) -> p b f", f=F)
        q_sb = area[:, 4 * BIG:5 * BIG].rearrange("p (b f) -> p b f", f=F)

        acc1 = area[:, 2 * BIG:2 * BIG + NBLK * (F + 1)].rearrange("p (b f) -> p b f", f=F + 1)
        hs = area[:, 3 * BIG + NBLK:3 * BIG + NBLK + NBLK * (F + 2)].rearrange("p (b f) -> p b f", f=F + 2)
        blk_all = area[:, 5 * BIG - NG:5 * BIG]

        cut = [0]

        def carve(n):
            a = area[:, cut[0]:cut[0] + n]
            cut[0] += n
            return a
        srcI = carve(T).bitcast(I32)
        dstI = carve(T).bitcast(I32)
        phi = carve(T)
        phi2 = carve(T)
        TB = T + 1
        keys = carve(2 * TB // 2 + 1).bitcast(BF16)[:, 0:2 * TB].rearrange("p (k t) -> p k t", k=2)
        los = carve(3 * TB // 2 + 1).bitcast(BF16)[:, 0:3 * TB].rearrange("p (k t) -> p k t", k=3)
        FILL = NG * JT // 64
        fillA = carve(FILL * RA).rearrange("p (r c) -> p r c", c=RA)
        fillB = carve(FILL * RB).rearrange("p (r c) -> p r c", c=RB)
        work_i = carve(T).bitcast(I32)
        assert cut[0] <= 5 * BIG and FILL * 64 == NG * JT

        PIECE = PT * P
        ring = sb("ring", [P, CHUNKS * SC * P + CHUNKS * SC * NBLK])
        ohlo = ring[:, 0:CHUNKS * SC * P].bitcast(BF16).rearrange("p (c t k n) -> p c t k n", c=CHUNKS, t=SC, k=2)
        ohkey = ring[:, CHUNKS * SC * P:CHUNKS * SC * (P + NBLK)].bitcast(BF16).rearrange(
            "p (c t k b) -> p c t k b", c=CHUNKS, t=SC, k=2)
        pos = sb("pos", [P, CHUNKS, SC, 2])
        posI = sb("posI", [P, CHUNKS, SC, 2], I32)
        trash = sb("trash", [P, 2, NBLK])
        rowB = sb("rowB", [P, CHUNKS, SC, RB])
        rec_area = sb("rec_area", [P, NPART * PT * RA])
        rowA = rec_area[:, 0:CHUNKS * SC * RA].rearrange("p (c t w) -> p c t w", c=CHUNKS, t=SC)
        rec = rec_area[:, :].rearrange("p (q t w) -> p q t w", q=NPART, t=PT)
        recB = sb("recB", [P, NPART, PT, RB])
        gat = sb("gat", [P, NPART, PT, 2 * F])
        oh = ring[:, 0:4 * PIECE].rearrange("p (r t n) -> p r t n", r=4, t=PT)
        ohT = ring[:, 4 * PIECE:5 * PIECE].rearrange("p (t n) -> p t n", t=PT)
        mask, scores, probs = oh[:, 0, :, :], ohT, oh[:, 1, :, :]
        nscore = ring[:, 2 * PIECE:4 * PIECE].rearrange("p (r n) -> p r n", r=2)
        nodes = sb("nodes", [P, NBLK, 2])
        pair = sb("pair", [P, PG, 2])
        other = sb("other", [P, PG, PG])
        cand = sb("cand", [P, PG, PG])
        gmax = sb("gmax", [P, PG])
        glow = sb("glow", [P, PG])
        lowest = sb("lowest", [P, PG])
        fall = sb("fall", [P, PG])
        fac = sb("fac", [P, 2, PG])
        work = sb("work", [P, 3 * PT * F])
        msg = work[:, 0:2 * PT * F].rearrange("p (r t f) -> p r t f", r=2, t=PT)
        msg2 = work[:, 2 * PT * F:3 * PT * F].rearrange("p (t f) -> p t f", t=PT)
        alpha = sb("alpha", [P, PT, HEADS])
        two = sb("two", [P, 2 * F])
        hT = sb("hT", [P, 2 * F])

        bank = [ctx.enter_context(nc.psum_tensor(f"bank{b}", [P, 512], F32)) for b in range(8)]

        def sems(name, n):
            return [sem(f"{name}{k}") for k in range(n)]

        s_iota = sem("s_iota")
        s_in = sem("s_in")
        s_xin = sem("s_xin")
        s_x0 = sem("s_x0")
        s_win = sem("s_win")
        s_w0 = sem("s_w0")
        s_const = sem("s_const")
        s_fillsrc = sem("s_fillsrc")
        s_fill = sem("s_fill")
        s_dve = sem("s_dve")
        s_ckey = sems("s_ckey", CHUNKS)
        s_cnt = sems("s_cnt", CHUNKS)
        s_start = sem("s_start")
        s_blki = sem("s_blki")
        s_blk = sem("s_blk")
        s_skey = sems("s_skey", CHUNKS)
        s_rank = sem("s_rank")
        s_read = sem("s_read")
        s_chunk = sems("s_chunk", CHUNKS)
        s_rows = sems("s_rows", CHUNKS)
        s_wld = sems("s_wld", CHUNKS)
        s_posf = sem("s_posf")
        s_pos = sems("s_pos", CHUNKS)
        s_go = sem("s_go")
        s_sc = sems("s_sc", CHUNKS)
        s_rec = sems("s_rec", NPART)
        s_gat = [sems("s_gat_early", NPART), sems("s_gat_late", NPART)]
        s_var = sem("s_var")
        s_root = sem("s_root")
        s_y = sem("s_y")
        s_tab = sem("s_tab")
        s_oh = sem("s_oh")
        s_agg = sem("s_agg")
        s_acc = sem("s_acc")
        s_msk = sem("s_msk")
        s_zt = sem("s_zt")
        s_pair = sem("s_pair")
        s_t = sem("s_t")
        s_l = sem("s_l")
        s_low = sem("s_low")
        s_p = sem("s_p")
        s_pt = sem("s_pt")
        s_ptc = sem("s_ptc")
        s_oT = sem("s_oT")
        s_oTc = sem("s_oTc")
        s_qg = sem("s_qg")
        s_m = sem("s_m")
        s_msg = sem("s_msg")
        s_two = sem("s_two")
        s_tr = sem("s_tr")
        s_trc = sem("s_trc")
        s_pr = sem("s_pr")
        s_prc = sem("s_prc")
        s_accd = sem("s_accd")
        s_out = sem("s_out")

        block = ctx.enter_context(nc.Block())

        PASSES = ["B", "A", "B", "B", "B", "A"]
        LAST = len(PASSES) - 1
        NPP = ITERS * NPART
        LOADS = [16 * (JT if l == 1 else 1) for l in range(len(PASSES))]
        LOADED = [sum(LOADS[:l]) * ITERS for l in range(len(PASSES))]
        fileA_v = fileA.rearrange("(g p j) c -> p g j c", p=P, j=JT)
        fileB_v = fileB.rearrange("(g p j) c -> p g j c", p=P, j=JT)

        def turns(eng, count, body, first=1, last=0):
            for i in range(first):
                body(i)
            with eng.Fori(first, count - last) as i:
                body(i)
            for i in range(count - last, count):
                body(i)

        def isfirst(i):
            return isinstance(i, int) and i == 0

        def part_before(i, q, k):
            return (i, q - k) if q >= k else None if isfirst(i) else (i - 1, q - k + NPART)

        def part_after(i, q, k):
            last = isinstance(i, int) and i == ITERS - 1
            return (i, q + k) if q + k < NPART else None if last else (i + 1, q + k - NPART)

        def node_rows(t):
            return t.rearrange("(b p) f -> p b f", p=P)

        @block.sync
        def _(sp):
            sp.dma_start(srcI, src.rearrange("(p t) -> p t", p=P)).then_inc(s_in, 16)
            sp.dma_start(dstI, dst.rearrange("(p t) -> p t", p=P)).then_inc(s_in, 16)
            sp.dma_start(phi, edge_weight.rearrange("(p t) -> p t", p=P)).then_inc(s_in, 16)
            sp.dma_start(phi2, edge_weight2.rearrange("(p t) -> p t", p=P)).then_inc(s_in, 16)
            sp.dma_start(wcols[:, 0, :], w_i.partition_broadcast(P)).then_inc(s_in, 16)
            sp.dma_start(wcols[:, 1, :], w_j.partition_broadcast(P)).then_inc(s_in, 16)
            sp.wait_ge(s_fillsrc, 1)
            fA = fileA.rearrange("(k p r) c -> k p r c", p=P, r=FILL)
            fB = fileB.rearrange("(k p r) c -> k p r c", p=P, r=FILL)
            for k in range(SLOTS // (P * FILL)):
                sp.dma_start(fA[k], fillA).then_inc(s_fill, 16)
                sp.dma_start(fB[k], fillB).then_inc(s_fill, 16)
            sp.wait_ge(s_w0, 1)
            for b in range(2):
                for hd in range(HEADS):
                    rows = slice(b * F + hd * D, b * F + hd * D + D)
                    cols = slice(hd * D, hd * D + D)
                    sp.dma_start(Wqk[rows, b, 0, cols], Wq[hd]).then_inc(s_win, 16)
                    sp.dma_start(Wqk[rows, b, 1, cols], Wk[hd]).then_inc(s_win, 16)
                    sp.dma_start(Wvb[rows, b, cols], Wv[hd]).then_inc(s_win, 16)
            ea = edge_attr.rearrange("(p t) f -> p t f", p=P)
            def load_chunks(i):
                for c in range(CHUNKS):
                    if not isfirst(i):
                        sp.wait_ge(s_sc[c], i * (2 * SC * 16))
                    sp.dma_start(rowA[:, c, :, 0:F], ea[:, bass.ds(i * (SC * CHUNKS) + c * SC, SC), :]).then_inc(s_wld[c], 16)

            turns(sp, TURNS, load_chunks)
            for c in range(CHUNKS):
                sp.wait_ge(s_sc[c], TURNS * 2 * SC * 16)
            sp.wait_ge(s_blki, 1)
            for k in range(2):
                sp.dma_start(blkfile[k:k + 1, :].rearrange("o (p j) -> (o p) j", p=P), blk_i[:, k, :]).then_inc(s_blk, 16)
            sp.wait_ge(s_blk, 32)
            sp.wait_ge(s_x0, 1)
            sp.dma_start(blk_all.bitcast(I32), blkfile[1, :].partition_broadcast(P)).then_inc(s_blk, 16)
            sp.dma_start(blkrow[:, :, :], blkfile.unsqueeze(0)).then_inc(s_blk, 16)
            sp.wait_ge(s_x0, 1)
            sp.dma_start(x_sb[:, 0:NBLK - 1, :], node_rows(x[0:(NBLK - 1) * P, :])).then_inc(s_xin, 16)
            sp.dma_start(x_sb[0:REST, NBLK - 1, :], x[(NBLK - 1) * P:N, :]).then_inc(s_xin, 16)

            for l, kind in enumerate(PASSES):
                sp.wait_ge(s_y, l + 1)
                tv = node_rows(table[l])
                if l == 0:
                    half = NBLK // 2
                    sp.dma_start(tv[:, 0:half, :], hs[:, 0:half, :]).then_inc(s_tab, 16)
                    sp.dma_start(tv[:, half:NBLK, :], hs[:, half:NBLK, :]).then_inc(s_tab, 16)
                elif l == LAST:
                    sp.dma_start(tv[:, :, 0:F], tmp).then_inc(s_tab, 16)
                    sp.dma_start(tv[:, :, F:2 * F], h_sb).then_inc(s_tab, 16)
                else:
                    sp.dma_start(tv[:, :, 0:F // 2], tmp[:, :, 0:F // 2]).then_inc(s_tab, 16)
                    sp.dma_start(tv[:, :, F // 2:F], tmp[:, :, F // 2:F]).then_inc(s_tab, 16)

                def load_parts(i):
                    for q in range(NPART):
                        if l > 0 or not isfirst(i):
                            sp.wait_ge(s_agg, i * NPART + (l * NPP + q + 1 - NPART))
                        g = i * (NPART * PG) + q * PG
                        if kind == "B":
                            sp.dma_start(recB[:, q, :, :].rearrange("p (g j) c -> p g (j c)", j=JT),
                                         fileB_v[:, bass.ds(g, PG), :, :].rearrange("p g j c -> p g (j c)")).then_inc(s_rec[q], 16)
                        elif l == LAST:
                            sp.dma_start(rec[:, q, :, :].rearrange("p (g j) c -> p g (j c)", j=JT),
                                         fileA_v[:, bass.ds(g, PG), :, :].rearrange("p g j c -> p g (j c)")).then_inc(s_rec[q], 16)
                        else:
                            for j in range(JT):
                                sp.dma_start(rec[:, q, :, F:RA].rearrange("p (g j) c -> p g j c", j=JT)[:, :, j, :],
                                             fileA_v[:, bass.ds(g, PG), j, F:RA]).then_inc(s_rec[q], 16)

                turns(sp, ITERS, load_parts, first=int(l == 0))
            sp.wait_ge(s_y, LAST + 2)
            sp.dma_start(node_rows(out[0:(NBLK - 1) * P, :]), x_sb[:, 0:NBLK - 1, :]).then_inc(s_out, 16)
            sp.dma_start(out[(NBLK - 1) * P:N, :], x_sb[0:REST, NBLK - 1, :]).then_inc(s_out, 16)
            sp.wait_ge(s_out, 32)

        @block.gpsimd
        def _(pool):
            nc.gpsimd.iota(iota_i[:, :], [[1, P]], base=0, channel_multiplier=0).then_inc(s_iota, 1)
            nc.gpsimd.iota(part_i[:, :], [[0, 1]], base=0, channel_multiplier=1).then_inc(s_iota, 1)
            nc.gpsimd.iota(gnum_i[:, :], [[1, NG // P]], base=0, channel_multiplier=NG // P).then_inc(s_iota, 1)
            pool.wait_ge(s_fill, 2 * 16 * (SLOTS // (P * FILL)))
            with pool.Fori(0, TURNS) as i:
                for c in range(CHUNKS):
                    pool.wait_ge(s_wld[c], i * 16 + 16)
                    pool.wait_ge(s_rows[c], i + 1)
                    pool.wait_ge(s_pos[c], i + 1)
                    pool.sem_inc(s_go, 1)
                    for t in range(SC):
                        pool.indirect_dma_start(fileA, bass.IndirectOffsetOnAxis(ap=posI[:, c, t, 0:1], axis=0),
                                                rowA[:, c, t, :], None).then_inc(s_sc[c], 16)
                        pool.indirect_dma_start(fileB, bass.IndirectOffsetOnAxis(ap=posI[:, c, t, 1:2], axis=0),
                                                rowB[:, c, t, :], None).then_inc(s_sc[c], 16)
            for l, kind in enumerate(PASSES):
                index = recB[:, :, :, 1:2] if kind == "B" else rec[:, :, :, A_IDX:A_IDX + 1]
                pool.wait_ge(s_tab, 32 * (l + 1))
                with pool.Fori(0, ITERS) as i:
                    for q in range(NPART):
                        pool.wait_ge(s_rec[q], i * LOADS[l] + (LOADED[l] + LOADS[l]))
                        pool.sem_inc(s_go, 1)
                        for t in range(PT):
                            pool.indirect_dma_start(gat[:, q, t, 0:TABW[l]], None, table[l], bass.IndirectOffsetOnAxis(
                                ap=index[:, q, t, :].bitcast(I32), axis=0)).then_inc(s_gat[l // 3][q], 16)

        @block.tensor
        def _(pe):
            cnt = [bank[0], bank[1]]
            rank = bank[2]
            deg = [bank[3], bank[4]]
            pe.wait_ge(s_const, 1)
            for k in range(2):
                nc.tensor.matmul(cnt[k][:, 0:SC * NBLK], ones_b[:, :], zeros_b[:, 0:SC * NBLK],
                                 start=True, stop=False, skip_group_check=True)
            with pe.Fori(0, TURNS) as i:
                for c in range(CHUNKS):
                    pe.wait_ge(s_ckey[c], i + 1)
                    for k in range(2):
                        mm = nc.tensor.matmul(cnt[k][:, 0:SC * NBLK], ones_b[:, :], ohkey[:, c, :, k, :],
                                              start=False, stop=False, skip_group_check=True)
                    mm.then_inc(s_cnt[c], 1)
            pe.wait_ge(s_start, 1)
            nc.tensor.matmul(rank[:, 0:2 * NBLK], ident[:, :], start_rows, start=True, stop=False, skip_group_check=True)
            for k in range(2):
                nc.tensor.matmul(deg[k][:, 0:NBLK], ones_b[:, :], zeros_b[:, 0:NBLK],
                                 start=True, stop=False, skip_group_check=True)
            with pe.Fori(0, TURNS) as i:
                for c in range(CHUNKS):
                    pe.wait_ge(s_skey[c], i + 1)
                    for t in range(SC):
                        nc.tensor.matmul(rank[:, 0:2 * NBLK], before[:, :], ohkey[:, c, t, :, :].rearrange("p k b -> p (k b)"),
                                         start=False, stop=False, skip_group_check=True).then_inc(s_rank, 1)
                        for k in range(2):
                            nc.tensor.matmul(deg[k][:, 0:NBLK], ohlo[:, c, t, k, :], ohkey[:, c, t, k, :],
                                             start=False, stop=False, skip_group_check=True)
                        pe.wait_ge(s_read, i * (CHUNKS * SC) + (c * SC + t + 1))
                        mm = nc.tensor.matmul(rank[:, 0:2 * NBLK], upto[:, :], ohkey[:, c, t, :, :].rearrange("p k b -> p (k b)"),
                                              start=False, stop=False, skip_group_check=True)
                    mm.then_inc(s_chunk[c], 1)

            def sums(l, i, q, left, right, width=F):
                for t in range(PT):
                    k = t // JT
                    mm = nc.tensor.matmul(bank[4 + q % 2][:, k * width:k * width + width], left[:, t, :], right[:, t, 0:width],
                                          start=(t % JT == 0), stop=(t % JT == JT - 1))
                mm.then_inc(s_agg, 1)

            def weighted_sums(i, q):
                pe.wait_ge(s_ptc, i * NPART + q + 1)
                sums(0, i, q, probs, gat[:, q, :, :], F + 1)

            def exponentials_back(i, q):
                pe.wait_ge(s_p, i * NPART + q + 1)
                for t in range(PT):
                    mm = nc.tensor.transpose(bank[2 + t // 4][:, t % 4 * P:t % 4 * P + P],
                                             nscore[:, q % 2, t * P:t * P + P], ident[:, :])
                mm.then_inc(s_pt, 1)

            def attend(i):
                for q in range(NPART):
                    if part_before(i, q, 2):
                        weighted_sums(*part_before(i, q, 2))
                    pe.wait_ge(s_msk, i * NPART + q + 1)
                    for t in range(PT):
                        mm = nc.tensor.transpose(bank[t // 4][:, t % 4 * P:t % 4 * P + P], scores[:, t, :], ident[:, :])
                    mm.then_inc(s_zt, 1)
                    if part_before(i, q, 1):
                        exponentials_back(*part_before(i, q, 1))

            turns(pe, ITERS, attend)
            weighted_sums(ITERS - 1, NPART - 2)
            exponentials_back(ITERS - 1, NPART - 1)
            weighted_sums(ITERS - 1, NPART - 1)
            for l in range(1, LAST):
                with pe.Fori(0, ITERS) as i:
                    for q in range(NPART):
                        pe.wait_ge(s_oh, i * NPART + (l * NPP + q + 1))
                        pe.wait_ge(s_gat[l // 3][q], i * (16 * PT) + (l % 3 * ITERS + 1) * 16 * PT)
                        sums(l, i, q, oh[:, q, :, :], gat[:, q, :, :])

            def project(weights, width, n0):
                def pair(i):
                    pe.wait_ge(s_two, i + (n0 + 1))
                    nc.tensor.transpose(bank[0][:, 0:P], two[:, :], ident[:, :]).then_inc(s_tr, 1)
                    pe.wait_ge(s_trc, i + (n0 + 1))
                    if n0 > 0 or not isfirst(i):
                        pe.wait_ge(s_prc, i + n0)
                    nc.tensor.matmul(bank[1][:, 0:width], hT[:, :], weights, start=True, stop=True).then_inc(s_pr, 1)

                turns(pe, NBLK // 2, pair)

            pe.wait_ge(s_win, 24 * 16)
            project(Wqk[:, :, :, :].rearrange("p b k f -> p (b k f)"), 4 * F, 0)
            pe.wait_ge(s_prc, NBLK // 2)
            breg = [pe.alloc_register(f"block{k}") for k in range(PG)]

            def ones_back(i, q):
                pe.wait_ge(s_oh, i * NPART + (LAST * NPP + q + 1))
                for t in range(PT):
                    mm = nc.tensor.transpose(bank[t // 4][:, t % 4 * P:t % 4 * P + P], oh[:, q, t, :], ident[:, :])
                mm.then_inc(s_oT, 1)

            def edge_queries(i, q):
                n = i * NPART + q
                pe.load(breg, blkrow[0:1, 0, bass.ds(i * (NPART * PG) + q * PG, PG)])
                blocks = [pe.snap(r, min_val=0, max_val=NBLK - 1) for r in breg]
                pe.wait_ge(s_oTc, n + 1)
                for t in range(PT):
                    mm = nc.tensor.matmul(bank[2][:, t * F:t * F + F], ohT[:, t, :],
                                          q_sb[:, bass.ds(blocks[t // JT], 1), :].rearrange("p b f -> p (b f)"),
                                          start=True, stop=True)
                mm.then_inc(s_qg, 1)

            def pairs(i):
                for q in range(NPART):
                    new, old = part_after(i, q, 1), part_before(i, q, 1)
                    if new:
                        ones_back(*new)
                    if old:
                        sums(LAST, *old, oh[:, old[1], :, :], msg[:, old[1] % 2, :, :])
                    pe.wait_ge(s_msg, i * NPART + q + 1)
                    if new:
                        edge_queries(*new)

            ones_back(0, 0)
            edge_queries(0, 0)
            turns(pe, ITERS, pairs, first=1, last=1)
            sums(LAST, ITERS - 1, NPART - 1, oh[:, NPART - 1, :, :], msg[:, (NPART - 1) % 2, :, :])
            project(Wvb[:, :, :].rearrange("p b f -> p (b f)"), 2 * F, NBLK // 2)

        @block.scalar
        def _(act):
            act.wait_ge(s_const, 1)
            def put_together(i):
                for c in range(CHUNKS):
                    if not isfirst(i):
                        act.wait_ge(s_sc[c], i * (2 * SC * 16))
                    cols = bass.ds(i * (SC * CHUNKS) + c * SC, SC)
                    nc.scalar.copy(rowA[:, c, :, A_LO], los[:, 2, cols])
                    nc.scalar.copy(rowA[:, c, :, A_LON], los[:, 0, cols])
                    nc.scalar.copy(rowA[:, c, :, A_PHI], phi[:, cols])
                    nc.scalar.copy(rowA[:, c, :, A_IDX].bitcast(I32), dstI[:, cols])
                    nc.scalar.copy(rowB[:, c, :, 0], los[:, 1, cols])
                    nc.scalar.copy(rowB[:, c, :, 1].bitcast(I32), srcI[:, cols]).then_inc(s_rows[c], 1)

            turns(act, TURNS, put_together)

            def root(n, rows):
                act.wait_ge(s_var, n)
                nc.scalar.activation(stat[:, rows, :], stat[:, rows, :], ACT.Sqrt).then_inc(s_root, 1)

            root(1, slice(0, 2))
            root(2, slice(1, 2))
            def exponentials(i, q):
                act.wait_ge(s_l, i * NPART + q + 1)
                nc.scalar.activation(fac[:, q % 2, :], fall[:, :], ACT.Exp)
                for k in range(PG):
                    g = nscore[:, q % 2, k * GROUP:k * GROUP + GROUP]
                    a = nc.scalar.activation(g, g, ACT.Exp, bias=lowest[:, k:k + 1])
                a.then_inc(s_p, 1)

            def exponentials_out(i, q, first=False):
                n = i * NPART + q
                act.wait_ge(s_pt, n + 1)
                if not first:
                    act.wait_ge(s_agg, n)
                for r in range(2):
                    a = nc.scalar.copy(probs[:, 4 * r:4 * r + 4, :].rearrange("p t n -> p (t n)"), bank[2 + r][:, :])
                a.then_inc(s_ptc, 1)

            def attend(i):
                for q in range(NPART):
                    n = i * NPART + q
                    if part_before(i, q, 2):
                        exponentials_out(*part_before(i, q, 2), first=isfirst(i) and q == 2)
                    act.wait_ge(s_oh, n + 1)
                    if part_before(i, q, 1):
                        act.wait_ge(s_zt, n)
                    act.wait_ge(s_gat[0][q], i * (16 * PT) + 16 * PT)
                    for t in range(PT):
                        a = nc.scalar.activation(scores[:, t, :], mask[:, t, :], ACT.Identity,
                                                 bias=gat[:, q, t, F + 1:F + 2], scale=-HUGE)
                    a.then_inc(s_msk, 1)
                    if part_before(i, q, 1):
                        exponentials(*part_before(i, q, 1))
                    act.wait_ge(s_zt, n + 1)
                    act.wait_ge(s_pair, n + 1)
                    for k in range(PG):
                        a = nc.scalar.activation(nscore[:, q % 2, k * GROUP:k * GROUP + GROUP],
                                                 bank[k // 2][:, k % 2 * GROUP:k % 2 * GROUP + GROUP],
                                                 ACT.Identity, bias=pair[:, k, 0:1])
                    a.then_inc(s_t, 1)

            turns(act, ITERS, attend)
            exponentials_out(ITERS - 1, NPART - 2)
            exponentials(ITERS - 1, NPART - 1)
            exponentials_out(ITERS - 1, NPART - 1)

            def project(source, n0):
                def pair(i):
                    nc.scalar.copy(two[:, :].rearrange("p (b f) -> p b f", b=2),
                                   source[:, bass.ds(i * 2, 2), :]).then_inc(s_two, 1)
                    act.wait_ge(s_tr, i + (n0 + 1))
                    if n0 > 0 or not isfirst(i):
                        act.wait_ge(s_pr, i + n0)
                    nc.scalar.copy(hT[:, :], bank[0][:, 0:P]).then_inc(s_trc, 1)

                turns(act, NBLK // 2, pair)

            root(3, slice(1, 2))
            root(4, slice(1, 2))
            root(5, slice(1, 2))
            act.wait_ge(s_m, 1)
            project(h_sb, 0)

            def ones_out(i):
                for q in range(NPART):
                    n = i * NPART + q
                    act.wait_ge(s_oT, n + 1)
                    if not (isfirst(i) and q == 0):
                        act.wait_ge(s_qg, n)
                    for b in range(2):
                        a = nc.scalar.copy(ohT[:, 4 * b:4 * b + 4, :].rearrange("p t n -> p (t n)"), bank[b][:, :])
                    a.then_inc(s_oTc, 1)

            turns(act, ITERS, ones_out)
            act.wait_ge(s_accd, 1)
            project(acc, NBLK // 2)

        @block.vector
        def _(v):
            done = [0]

            def nth():
                done[0] += 1
                return done[0]

            v.wait_ge(s_iota, 3)
            nc.vector.tensor_copy(iota[:, :], iota_i[:, :]).then_inc(s_dve, 1)
            v.wait_ge(s_dve, nth())
            nc.vector.tensor_copy(part[:, :], part_i[:, :]).then_inc(s_dve, 1)
            v.wait_ge(s_dve, nth())
            nc.vector.tensor_copy(gnum[:, :], gnum_i[:, :])
            nc.vector.tensor_copy(iota_b[:, :], iota_i[:, :])
            nc.vector.tensor_scalar(ident[:, :], iota[:, :], part[:, 0:1], None, ALU.is_equal)
            nc.vector.tensor_scalar(before[:, :], iota[:, :], part[:, 0:1], None, ALU.is_gt)
            nc.vector.tensor_scalar(upto[:, :], iota[:, :], part[:, 0:1], None, ALU.is_le)
            nc.vector.memset(ones_b[:, :], 1.0)
            nc.vector.memset(zeros_b[:, :], 0.0)
            nc.vector.memset(Wqk[:, :, :, :], 0.0)
            nc.vector.memset(Wvb[:, :, :], 0.0).then_inc(s_w0, 1)
            nc.vector.memset(fillA[:, :, :], 0.0)
            nc.vector.memset(fillB[:, :, :], 0.0).then_inc(s_dve, 1)
            v.wait_ge(s_dve, nth())
            nc.vector.memset(fillA[:, :, A_LO:A_LON + 1], -1.0)
            nc.vector.memset(fillB[:, :, 0:1], -1.0).then_inc(s_fillsrc, 1)
            v.wait_ge(s_in, 6 * 16)
            for k, ends in enumerate((srcI, dstI)):
                nc.vector.tensor_single_scalar(work_i, ends, 7, ALU.arith_shift_right).then_inc(s_dve, 1)
                v.wait_ge(s_dve, nth())
                nc.vector.tensor_copy(keys[:, k, 0:T], work_i).then_inc(s_dve, 1)
                v.wait_ge(s_dve, nth())
                nc.vector.tensor_single_scalar(work_i, ends, P - 1, ALU.bitwise_and).then_inc(s_dve, 1)
                v.wait_ge(s_dve, nth())
                nc.vector.tensor_copy(los[:, 2 - k, 0:T], work_i).then_inc(s_dve, 1)
                v.wait_ge(s_dve, nth())
            nc.vector.tensor_tensor(phi, phi, phi2, ALU.mult)
            nc.vector.tensor_tensor(work_i.bitcast(F32), srcI, dstI, ALU.not_equal)
            nc.vector.tensor_scalar(los[:, 0, 0:T], los[:, 2, 0:T], 1.0, None, ALU.add).then_inc(s_dve, 1)
            v.wait_ge(s_dve, nth())
            nc.vector.tensor_tensor(los[:, 0, 0:T], los[:, 0, 0:T], work_i.bitcast(F32), ALU.mult).then_inc(s_dve, 1)
            v.wait_ge(s_dve, nth())
            nc.vector.tensor_scalar(los[:, 0, 0:T], los[:, 0, 0:T], -1.0, None, ALU.add).then_inc(s_const, 1)
            v.wait_ge(s_const, 1)

            def ones_by_block(c, i):
                cols = bass.ds(i * (SC * CHUNKS) + c * SC, SC)
                for k in range(2):
                    last = nc.vector.tensor_tensor(
                        ohkey[:, c, :, k, :], iota_b[:, 0:NBLK].unsqueeze(1).broadcast_to((P, SC, NBLK)),
                        keys[:, k, cols].unsqueeze(2).broadcast_to((P, SC, NBLK)), ALU.is_equal)
                return last

            def count(i):
                for c in range(CHUNKS):
                    if not isfirst(i):
                        v.wait_ge(s_cnt[c], i)
                    ones_by_block(c, i).then_inc(s_ckey[c], 1)

            turns(v, TURNS, count)
            for c in range(CHUNKS):
                v.wait_ge(s_cnt[c], TURNS)
            for k in range(2):
                nc.vector.tensor_reduce(cntf[:, k, :], bank[k][:, 0:SC * NBLK].rearrange("p (t b) -> p b t", t=SC),
                                        AX.X, ALU.add).then_inc(s_dve, 1)
                v.wait_ge(s_dve, nth())
            nc.vector.tensor_scalar(cnti[:, :, :], cntf[:, :, :], float(GROUP - 1), None, ALU.add).then_inc(s_dve, 1)
            v.wait_ge(s_dve, nth())
            nc.vector.tensor_single_scalar(cnti[:, :, :], cnti[:, :, :], GROUP.bit_length() - 1,
                                           ALU.arith_shift_right).then_inc(s_dve, 1)
            v.wait_ge(s_dve, nth())
            nc.vector.tensor_copy(cntf[:, :, :], cnti[:, :, :]).then_inc(s_dve, 1)
            v.wait_ge(s_dve, nth())
            for k in range(2):
                nc.vector.tensor_tensor_scan(start[:, k, :], cntf[:, k, :], zeros_b[:, 0:NBLK], 0.0, ALU.add, ALU.add).then_inc(s_dve, 1)
                v.wait_ge(s_dve, nth())
            nc.vector.tensor_tensor(start[:, :, :], start[:, :, :], cntf[:, :, :], ALU.subtract).then_inc(s_dve, 1)
            v.wait_ge(s_dve, nth())
            nc.vector.tensor_scalar(start_rows, start[:, :, :].rearrange("p k b -> p (k b)"), float(GROUP), None,
                                    ALU.mult).then_inc(s_start, 1)
            GC = NG // P
            for k in range(2):
                cmp = ring[:, 0:GC * NBLK].rearrange("p (g b) -> p g b", b=NBLK)
                nc.vector.tensor_tensor(cmp, start[:, k, :].unsqueeze(1).broadcast_to((P, GC, NBLK)),
                                        gnum[:, :].unsqueeze(2).broadcast_to((P, GC, NBLK)), ALU.is_le).then_inc(s_dve, 1)
                v.wait_ge(s_dve, nth())
                nc.vector.tensor_reduce(trash[:, 0, 0:GC], cmp, AX.X, ALU.add).then_inc(s_dve, 1)
                v.wait_ge(s_dve, nth())
                nc.vector.tensor_scalar(blk_i[:, k, :], trash[:, 0, 0:GC], -1.0, None, ALU.add).then_inc(s_dve, 1)
                v.wait_ge(s_dve, nth())
            v.sem_inc(s_blki, 1)

            def sort(i):
                for c in range(CHUNKS):
                    if not isfirst(i):
                        v.wait_ge(s_chunk[c], i)
                    ones_by_block(c, i)
                    cols = bass.ds(i * (SC * CHUNKS) + c * SC, SC)
                    for k in range(2):
                        last = nc.vector.tensor_tensor(
                            ohlo[:, c, :, k, :], iota_b[:, :].unsqueeze(1).broadcast_to((P, SC, P)),
                            los[:, k, cols].unsqueeze(2).broadcast_to((P, SC, P)), ALU.is_equal)
                    last.then_inc(s_skey[c], 1)
                    v.wait_ge(s_skey[c], i + 1)
                    for t in range(SC):
                        v.wait_ge(s_rank, i * (CHUNKS * SC) + (c * SC + t + 1))
                        for k in range(2):
                            last = nc.vector.tensor_tensor_reduce(
                                trash[:, k, :], ohkey[:, c, t, k, :], bank[2][:, k * NBLK:k * NBLK + NBLK],
                                1.0, 0.0, ALU.mult, ALU.add, pos[:, c, t, k:k + 1])
                        last.then_inc(s_read, 1)
                    v.wait_ge(s_read, i * (CHUNKS * SC) + (c * SC + SC))
                    if not isfirst(i):
                        v.wait_ge(s_sc[c], i * (2 * SC * 16))
                    nc.vector.tensor_copy(posI[:, c, :, :], pos[:, c, :, :]).then_inc(s_pos[c], 1)

            turns(v, TURNS, sort)
            for c in range(CHUNKS):
                v.wait_ge(s_chunk[c], TURNS)
            for k in range(2):
                nc.vector.tensor_copy(degs[:, k, :], bank[3 + k][:, 0:NBLK]).then_inc(s_dve, 1)
                v.wait_ge(s_dve, nth())
            nc.vector.tensor_scalar(stat[:, 0, :], degs[:, 0, :], 1.0, None, ALU.add)
            nc.vector.tensor_scalar(stat[:, 1, :], degs[:, 1, :], 1.0, None, ALU.max).then_inc(s_var, 1)
            v.wait_ge(s_root, 1)
            nc.vector.reciprocal(dinv1[:, :], stat[:, 0, :]).then_inc(s_dve, 1)
            v.wait_ge(s_dve, nth())
            nc.vector.reciprocal(dinv2[:, :], stat[:, 1, :]).then_inc(s_dve, 1)
            v.wait_ge(s_dve, nth())
            nc.vector.tensor_scalar(trash[:, 0, :], degs[:, 1, :], 0.0, None, ALU.is_gt).then_inc(s_dve, 1)
            v.wait_ge(s_dve, nth())
            nc.vector.tensor_tensor(dinv2[:, :], dinv2[:, :], trash[:, 0, :], ALU.mult).then_inc(s_dve, 1)
            v.wait_ge(s_dve, nth())
            for c in range(CHUNKS):
                v.wait_ge(s_sc[c], TURNS * 2 * SC * 16)
            nc.vector.memset(x_sb[:, NBLK - 1, :], 0.0).then_inc(s_x0, 1)
            v.wait_ge(s_xin, 32)

            def by_node(col):
                return col.unsqueeze(2).broadcast_to((P, NBLK, F))

            roots = [1]

            def layernorm():
                nc.vector.tensor_reduce(stat[:, 0, :], x_sb, AX.X, ALU.add).then_inc(s_dve, 1)
                v.wait_ge(s_dve, nth())
                nc.vector.tensor_scalar(stat[:, 0, :], stat[:, 0, :], -1.0 / F, None, ALU.mult).then_inc(s_dve, 1)
                v.wait_ge(s_dve, nth())
                nc.vector.tensor_tensor(tmp, x_sb, by_node(stat[:, 0, :]), ALU.add).then_inc(s_dve, 1)
                v.wait_ge(s_dve, nth())
                nc.vector.tensor_tensor(h_sb, tmp, tmp, ALU.mult).then_inc(s_dve, 1)
                v.wait_ge(s_dve, nth())
                nc.vector.tensor_reduce(stat[:, 1, :], h_sb, AX.X, ALU.add).then_inc(s_dve, 1)
                v.wait_ge(s_dve, nth())
                nc.vector.tensor_scalar(stat[:, 1, :], stat[:, 1, :], 1.0 / F, EPS, ALU.mult, ALU.add).then_inc(s_var, 1)
                roots[0] += 1
                v.wait_ge(s_root, roots[0])
                nc.vector.reciprocal(stat[:, 1, :], stat[:, 1, :]).then_inc(s_dve, 1)
                v.wait_ge(s_dve, nth())
                nc.vector.tensor_tensor(h_sb, tmp, by_node(stat[:, 1, :]), ALU.mult).then_inc(s_dve, 1)
                v.wait_ge(s_dve, nth())
                nc.vector.tensor_scalar(h_sb, h_sb, 0.0, None, ALU.max).then_inc(s_dve, 1)
                v.wait_ge(s_dve, nth())

            breg = [v.alloc_register(f"vblock{k}") for k in range(PG)]

            def load_blocks(kind, i, q):
                which = 0 if kind == "A" else 1
                v.load(breg, blkrow[0:1, which, bass.ds(i * (NPART * PG) + q * PG, PG)])
                return [v.snap(r, min_val=0, max_val=NBLK - 1) for r in breg]

            def ones_by_node(names, op, q):
                nc.vector.tensor_tensor(oh[:, q, :, :], iota[:, :].unsqueeze(1).broadcast_to((P, PT, P)),
                                        names.unsqueeze(2).broadcast_to((P, PT, P)), op).then_inc(s_oh, 1)

            v.wait_ge(s_blk, 64)
            layernorm()
            for k in range(2):
                nc.vector.tensor_tensor(tmp, h_sb, wcols[:, k, :].unsqueeze(1).broadcast_to((P, NBLK, F)), ALU.mult).then_inc(s_dve, 1)
                v.wait_ge(s_dve, nth())
                nc.vector.tensor_reduce(stat[:, k, :], tmp, AX.X, ALU.add).then_inc(s_dve, 1)
                v.wait_ge(s_dve, nth())
            nc.vector.tensor_copy(blk_all, blk_all.bitcast(I32)).then_inc(s_dve, 1)
            v.wait_ge(s_dve, nth())
            nc.vector.tensor_tensor(trash[:, 0, :], stat[:, 0, :], stat[:, 1, :], ALU.add).then_inc(s_dve, 1)
            v.wait_ge(s_dve, nth())
            nc.vector.scalar_tensor_tensor(trash[:, 1, :], trash[:, 0, :], 0.01, trash[:, 0, :], ALU.mult, ALU.max).then_inc(s_dve, 1)
            v.wait_ge(s_dve, nth())
            nc.vector.tensor_scalar(nodes[:, :, 1], trash[:, 1, :], -1.0, None, ALU.mult)
            nc.vector.tensor_copy(nodes[:, :, 0], stat[:, 0, :])
            nc.vector.memset(acc1[:, :, F:F + 1], 1.0)
            nc.vector.tensor_copy(acc1[:, :, 0:F], h_sb)
            nc.vector.memset(hs[:, :, F:F + 1], 1.0)
            nc.vector.tensor_copy(hs[:, :, F + 1], stat[:, 1, :])
            nc.vector.tensor_copy(hs[:, :, 0:F], h_sb).then_inc(s_dve, 1)
            v.wait_ge(s_dve, nth())
            v.sem_inc(s_y, 1)

            def masks(i, q):
                n = i * NPART + q
                v.wait_ge(s_rec[q], i * 16 + 16)
                if not (isinstance(n, int) and n == 0):
                    v.wait_ge(s_msk, n)
                nc.vector.tensor_tensor(mask, iota[:, :].unsqueeze(1).broadcast_to((P, PT, P)),
                                        recB[:, q, :, 0].unsqueeze(2).broadcast_to((P, PT, P)), ALU.not_equal).then_inc(s_oh, 1)

            def maxima(i, q):
                n = i * NPART + q
                STEPS = 11
                g = i * (NPART * PG) + q * PG
                b = load_blocks("B", i, q)
                mine = blk_all[:, bass.ds(g, PG)]
                nc.vector.tensor_tensor(other[:, :, :], mine.unsqueeze(2).broadcast_to((P, PG, PG)),
                                        mine.unsqueeze(1).broadcast_to((P, PG, PG)), ALU.not_equal).then_inc(s_low, 1)
                v.wait_ge(s_t, n + 1)
                e = nscore[:, q % 2, :]
                nc.vector.scalar_tensor_tensor(e, e, 0.01, e, ALU.mult, ALU.max).then_inc(s_low, 1)
                v.wait_ge(s_low, n * STEPS + 2)
                nc.vector.tensor_reduce(gmax[:, :], e.rearrange("p (k e) -> p k e", k=PG), AX.X, ALU.max).then_inc(s_low, 1)
                v.wait_ge(s_low, n * STEPS + 3)
                nc.vector.scalar_tensor_tensor(cand[:, :, :], other[:, :, :], HUGE, gmax[:, :].unsqueeze(1).broadcast_to((P, PG, PG)),
                                               ALU.mult, ALU.subtract).then_inc(s_low, 1)
                v.wait_ge(s_low, n * STEPS + 4)
                nc.vector.tensor_reduce(glow[:, :], cand[:, :, :], AX.X, ALU.min).then_inc(s_low, 1)
                v.wait_ge(s_low, n * STEPS + 5)
                nc.vector.tensor_tensor(lowest[:, :], glow[:, :], pair[:, :, 1], ALU.min).then_inc(s_low, 1)
                v.wait_ge(s_low, n * STEPS + 6)
                nc.vector.tensor_tensor(fall[:, :], lowest[:, :], pair[:, :, 1], ALU.subtract).then_inc(s_low, 1)
                v.wait_ge(s_low, n * STEPS + 7)
                after_first = other[:, :, :].rearrange("p k j -> p (k j)")[:, PG:PG * PG:PG + 1]
                nc.vector.tensor_tensor(fall[:, 1:PG], fall[:, 1:PG], after_first, ALU.mult).then_inc(s_l, 1)
                for k in range(PG):
                    nc.vector.tensor_scalar(nodes[:, bass.ds(b[k], 1), 1], lowest[:, k:k + 1], 1.0, None, ALU.mult).then_inc(s_low, 1)
                    v.wait_ge(s_low, n * STEPS + (8 + k))

            def add_weighted(i, q):
                n = i * NPART + q
                b = load_blocks("B", i, q)
                v.wait_ge(s_agg, n + 1)
                W = F + 1
                for k in range(PG):
                    here = acc1[:, bass.ds(b[k], 1), :].rearrange("p b f -> p (b f)")
                    nc.vector.scalar_tensor_tensor(here, here, fac[:, q % 2, k:k + 1], bank[4 + q % 2][:, k * W:k * W + W],
                                                   ALU.mult, ALU.add).then_inc(s_acc, 1)
                    v.wait_ge(s_acc, n * PG + (k + 1))

            def attend(i):
                for q in range(NPART):
                    n = i * NPART + q
                    if part_before(i, q, 1):
                        maxima(*part_before(i, q, 1))
                        v.wait_ge(s_l, n)
                    b = load_blocks("B", i, q)
                    for k in range(PG):
                        a = nc.vector.tensor_copy(pair[:, k, :], nodes[:, bass.ds(b[k], 1), :].rearrange("p b c -> p (b c)"))
                    a.then_inc(s_pair, 1)
                    if part_before(i, q, 2):
                        add_weighted(*part_before(i, q, 2))
                    if part_after(i, q, 1):
                        masks(*part_after(i, q, 1))

            masks(0, 0)
            turns(v, ITERS, attend, last=1)
            maxima(ITERS - 1, NPART - 1)
            add_weighted(ITERS - 1, NPART - 2)
            add_weighted(ITERS - 1, NPART - 1)
            nc.vector.reciprocal(stat[:, 3, :], acc1[:, :, F]).then_inc(s_dve, 1)
            v.wait_ge(s_dve, nth())
            nc.vector.tensor_tensor(h_sb, acc1[:, :, 0:F], by_node(stat[:, 3, :]), ALU.mult).then_inc(s_dve, 1)
            v.wait_ge(s_dve, nth())
            nc.vector.scalar_tensor_tensor(x_sb, h_sb, 0.0, x_sb, ALU.max, ALU.add).then_inc(s_dve, 1)
            v.wait_ge(s_dve, nth())

            def plain(l, names):
                with v.Fori(0, ITERS) as i:
                    for q in range(NPART):
                        n = i * NPART + (l * NPP + q)
                        b = load_blocks(PASSES[l], i, q)
                        v.wait_ge(s_rec[q], i * LOADS[l] + (LOADED[l] + LOADS[l]))
                        ones_by_node(names[:, q, :], ALU.is_equal, q)
                        v.wait_ge(s_agg, n + 1)
                        add_sums(l, n, q, b)

            def add_sums(l, n, q, b):
                for k in range(PG):
                    here = acc[:, bass.ds(b[k], 1), :].rearrange("p b f -> p (b f)")
                    nc.vector.tensor_tensor(here, here, bank[4 + q % 2][:, k * F:k * F + F], ALU.add).then_inc(s_acc, 1)
                    v.wait_ge(s_acc, n * PG + (k + 1))

            layernorm()
            nc.vector.tensor_tensor(tmp, h_sb, by_node(dinv1[:, :]), ALU.mult).then_inc(s_dve, 1)
            v.wait_ge(s_dve, nth())
            nc.vector.tensor_copy(acc, tmp).then_inc(s_dve, 1)
            v.wait_ge(s_dve, nth())
            v.sem_inc(s_y, 1)
            plain(1, rec[:, :, :, A_LON])
            nc.vector.tensor_tensor(acc, acc, by_node(dinv1[:, :]), ALU.mult).then_inc(s_dve, 1)
            v.wait_ge(s_dve, nth())
            nc.vector.tensor_tensor(x_sb, x_sb, acc, ALU.add).then_inc(s_dve, 1)
            v.wait_ge(s_dve, nth())

            layernorm()
            nc.vector.tensor_copy(q_sb, h_sb)
            nc.vector.tensor_tensor(tmp, h_sb, by_node(dinv2[:, :]), ALU.mult).then_inc(s_dve, 1)
            v.wait_ge(s_dve, nth())
            for l in range(2, LAST):
                nc.vector.memset(acc, 0.0).then_inc(s_dve, 1)
                v.wait_ge(s_dve, nth())
                v.sem_inc(s_y, 1)
                plain(l, recB[:, :, :, 0])
                nc.vector.tensor_tensor(acc, acc, by_node(dinv2[:, :]), ALU.mult).then_inc(s_dve, 1)
                v.wait_ge(s_dve, nth())
                nc.vector.tensor_tensor(q_sb, q_sb, acc, ALU.add).then_inc(s_dve, 1)
                v.wait_ge(s_dve, nth())
                nc.vector.tensor_tensor(tmp, acc, by_node(dinv2[:, :]), ALU.mult).then_inc(s_dve, 1)
                v.wait_ge(s_dve, nth())
            nc.vector.scalar_tensor_tensor(x_sb, q_sb, 0.25, x_sb, ALU.mult, ALU.add).then_inc(s_dve, 1)
            v.wait_ge(s_dve, nth())

            layernorm()
            nc.vector.memset(acc, 0.0).then_inc(s_dve, 1)
            v.wait_ge(s_dve, nth())
            v.sem_inc(s_m, 1)
            with v.Fori(0, NBLK // 2) as i:
                v.wait_ge(s_pr, i + 1)
                both = bank[1][:, 0:4 * F].rearrange("p (b k f) -> p b k f", b=2, k=2)
                nc.vector.tensor_copy(q_sb[:, bass.ds(i * 2, 2), :], both[:, :, 0, :])
                nc.vector.tensor_copy(tmp[:, bass.ds(i * 2, 2), :], both[:, :, 1, :]).then_inc(s_prc, 1)
            v.wait_ge(s_prc, NBLK // 2)
            v.sem_inc(s_y, 1)
            SCALE = float(D) ** -0.5

            def pair_ones(i, q):
                v.wait_ge(s_rec[q], i * 16 + (LOADED[LAST] + 16))
                ones_by_node(rec[:, q, :, A_LO], ALU.is_equal, q)

            def pairs(i):
                STEPS = 4
                for q in range(NPART):
                    n = i * NPART + q
                    v.wait_ge(s_gat[LAST // 3][q], i * (16 * PT) + (LAST % 3 * ITERS + 1) * 16 * PT)
                    nc.vector.tensor_tensor(msg2, rec[:, q, :, 0:F], gat[:, q, :, 0:F], ALU.mult).then_inc(s_m, 1)
                    v.wait_ge(s_m, n * STEPS + 2)
                    v.wait_ge(s_qg, n + 1)
                    nc.vector.tensor_tensor(msg2, msg2, bank[2][:, 0:PT * F].rearrange("p (t f) -> p t f", t=PT), ALU.mult).then_inc(s_m, 1)
                    v.wait_ge(s_m, n * STEPS + 3)
                    nc.vector.tensor_reduce(alpha[:, :, :], msg2.rearrange("p t (h d) -> p t h d", h=HEADS), AX.X, ALU.add).then_inc(s_m, 1)
                    v.wait_ge(s_m, n * STEPS + 4)
                    nc.vector.scalar_tensor_tensor(alpha[:, :, :], alpha[:, :, :], SCALE,
                                                   rec[:, q, :, A_PHI].unsqueeze(2).broadcast_to((P, PT, HEADS)),
                                                   ALU.mult, ALU.mult).then_inc(s_m, 1)
                    v.wait_ge(s_m, n * STEPS + 5)
                    nc.vector.tensor_tensor(msg[:, q % 2, :, :].rearrange("p t (h d) -> p t h d", h=HEADS),
                                            gat[:, q, :, F:2 * F].rearrange("p t (h d) -> p t h d", h=HEADS),
                                            alpha[:, :, :].unsqueeze(3).broadcast_to((P, PT, HEADS, D)), ALU.mult).then_inc(s_msg, 1)
                    if part_after(i, q, 2):
                        pair_ones(*part_after(i, q, 2))
                    if part_before(i, q, 1):
                        add_pairs(*part_before(i, q, 1))

            def add_pairs(i, q):
                n = i * NPART + (LAST * NPP + q)
                b = load_blocks("A", i, q)
                v.wait_ge(s_agg, n + 1)
                add_sums(LAST, n, q, b)

            pair_ones(0, 0)
            pair_ones(0, 1)
            turns(v, ITERS, pairs, first=1, last=1)
            add_pairs(ITERS - 1, NPART - 1)
            v.sem_inc(s_accd, 1)
            with v.Fori(0, NBLK // 2) as i:
                v.wait_ge(s_pr, i + (NBLK // 2 + 1))
                xs = x_sb[:, bass.ds(i * 2, 2), :]
                nc.vector.tensor_tensor(xs, xs, bank[1][:, 0:2 * F].rearrange("p (b f) -> p b f", b=2), ALU.add).then_inc(s_prc, 1)
            v.wait_ge(s_prc, NBLK)
            v.sem_inc(s_y, 1)


_INS = ["x", "src", "dst", "edge_attr_64", "edge_weight", "edge_weight_n2",
        "L0_gnn_w_i", "L0_gnn_w_j", "L3_gnn_Wq", "L3_gnn_Wk", "L3_gnn_Wv"]


def kernel(**inputs):
    import numpy as np
    import concourse.bacc as bacc
    from concourse import mybir as mb
    from concourse.bass_utils import run_bass_kernel_spmd

    nc = bacc.Bacc("TRN2", target_bir_lowering=False, num_devices=1)
    arrays, args = {}, []
    for name in _INS:
        a = np.ascontiguousarray(inputs[name])
        arrays[f"in_{name}"] = a
        args.append(nc.dram_tensor(f"in_{name}", a.shape, mb.dt.from_np(a.dtype), kind="ExternalInput").ap())
    args.append(nc.dram_tensor("out_x", inputs["x"].shape, mb.dt.float32, kind="ExternalOutput").ap())
    gnn_four_layers(nc, *args)
    r = run_bass_kernel_spmd(nc, [arrays], core_ids=[0])
    return r.results[0]["out_x"]
```

```python
from contextlib import ExitStack

import concourse.bass as bass
from concourse import mybir

ALU = mybir.AluOpType
ACT = mybir.ActivationFunctionType
F32 = mybir.dt.float32
BF16 = mybir.dt.bfloat16
I32 = mybir.dt.int32
AX = mybir.AxisListType

P = 128
HUGE = 1.0e30


def gnn_four_layers(nc, x, src, dst, edge_attr, edge_weight, edge_weight2, w_i, w_j, Wq, Wk, Wv, out):
    N, F = x.shape
    E = src.shape[0]
    HEADS, D, _ = Wq.shape
    EPS = 1e-5
    NBLK = -(-N // P)
    REST = N - (NBLK - 1) * P
    ROWS = NBLK * P

    JT = 2
    GROUP = JT * P
    PT, PG = 8, 4
    NPART = 4
    most = E // GROUP + NBLK
    ITERS = -(-most // (NPART * PG))
    NG = ITERS * NPART * PG
    SLOTS = NG * GROUP
    RA = F + 4
    A_LO, A_LON, A_PHI, A_IDX = F, F + 1, F + 2, F + 3
    RB = 2

    T = E // P
    SC = 5
    CHUNKS = 5
    TURNS = T // (SC * CHUNKS)
    assert T * P == E and TURNS * SC * CHUNKS == T and D * HEADS == F

    fileA = nc.dram_tensor("fileA", (SLOTS, RA), F32, kind="Internal").ap()
    fileB = nc.dram_tensor("fileB", (SLOTS + E + GROUP, RB), F32, kind="Internal").ap()
    blkfile = nc.dram_tensor("blkfile", (3, NG), I32, kind="Internal").ap()
    TABW = [F + 2, F, F, F, F, 2 * F]
    table = [nc.dram_tensor(f"table{l}", (ROWS, w), F32, kind="Internal").ap() for l, w in enumerate(TABW)]

    with ExitStack() as ctx:
        def sb(name, shape, dt=F32):
            return ctx.enter_context(nc.sbuf_tensor(name, shape, dt))

        def sem(name):
            return ctx.enter_context(nc.semaphore(name))

        iota_i = sb("iota_i", [P, P], I32)
        part_i = sb("part_i", [P, 1], I32)
        iota = sb("iota", [P, P])
        part = sb("part", [P, 1])
        iota_b = sb("iota_b", [P, P], BF16)
        ident = sb("ident", [P, P])
        before = sb("before", [P, P], BF16)
        upto = sb("upto", [P, P], BF16)
        ones_b = sb("ones_b", [P, P], BF16)
        blkrow = sb("blkrow", [1, 2, NG], I32)
        blk_i = sb("blk_i", [P, 3, NG // P], I32)
        next_i = sb("next_i", [P, 1], I32)
        next_f = sb("next_f", [P, 1])
        rising = sb("rising", [P, 1])
        unsorted = sb("unsorted", [P, 1], BF16)
        in_order = sb("in_order", [P, 1])
        in_order_i = sb("in_order_i", [P, 1], I32)
        wcols = sb("wcols", [P, 2, F])
        Wqk = sb("Wqk", [P, 2, 2, F])
        Wvb = sb("Wvb", [P, 2, F])
        degs = sb("degs", [P, 2, NBLK])
        dinv1 = sb("dinv1", [P, NBLK])
        dinv2 = sb("dinv2", [P, NBLK])
        stat = sb("stat", [P, 4, NBLK])
        start = sb("start", [P, 2, NBLK])
        start_r = sb("start_r", [P, 2, NBLK])
        start_rows = start_r[:, :, :].rearrange("p k b -> p (k b)")
        cntf = sb("cntf", [P, 2, NBLK])
        cnti = sb("cnti", [P, 2, NBLK], I32)
        gnum = sb("gnum", [P, NG // P])
        gnum_i = sb("gnum_i", [P, NG // P], I32)
        zeros_b = sb("zeros_b", [P, 512], BF16)

        BIG = NBLK * F
        area = sb("area", [P, 5 * BIG])
        x_sb = area[:, 0:BIG].rearrange("p (b f) -> p b f", f=F)
        h_sb = area[:, BIG:2 * BIG].rearrange("p (b f) -> p b f", f=F)
        acc = area[:, 2 * BIG:3 * BIG].rearrange("p (b f) -> p b f", f=F)
        tmp = area[:, 3 * BIG:4 * BIG].rearrange("p (b f) -> p b f", f=F)
        q_sb = area[:, 4 * BIG:5 * BIG].rearrange("p (b f) -> p b f", f=F)

        acc1 = area[:, 2 * BIG:2 * BIG + NBLK * (F + 1)].rearrange("p (b f) -> p b f", f=F + 1)
        hs = area[:, 3 * BIG + NBLK:3 * BIG + NBLK + NBLK * (F + 2)].rearrange("p (b f) -> p b f", f=F + 2)
        node0 = area[:, 5 * BIG - NG:5 * BIG]
        rowrow = area[0:1, 5 * BIG - 2 * NG:5 * BIG - NG].bitcast(I32)

        cut = [0]

        def carve(n):
            a = area[:, cut[0]:cut[0] + n]
            cut[0] += n
            return a
        srcI = carve(T).bitcast(I32)
        dstI = carve(T).bitcast(I32)
        phi = carve(T)
        TB = T + 1
        keys = carve(2 * TB // 2 + 1).bitcast(BF16)[:, 0:2 * TB].rearrange("p (k t) -> p k t", k=2)
        los = carve(3 * TB // 2 + 1).bitcast(BF16)[:, 0:3 * TB].rearrange("p (k t) -> p k t", k=3)
        FILL = NG * JT // 64
        fillA = carve(FILL * RA).rearrange("p (r c) -> p r c", c=RA)
        fillB = carve(FILL * RB).rearrange("p (r c) -> p r c", c=RB)
        ends = carve(2 * T)
        phi2 = ends[:, 0:T]
        work_i = ends[:, T:2 * T].bitcast(I32)
        ends = ends.rearrange("p (t c) -> p t c", c=RB)
        assert cut[0] <= 5 * BIG and FILL * 64 == NG * JT

        PIECE = PT * P
        ring = sb("ring", [P, CHUNKS * SC * P + CHUNKS * SC * NBLK])
        ohlo = ring[:, 0:CHUNKS * SC * P].bitcast(BF16).rearrange("p (c t k n) -> p c t k n", c=CHUNKS, t=SC, k=2)
        ohkey = ring[:, CHUNKS * SC * P:CHUNKS * SC * (P + NBLK)].bitcast(BF16).rearrange(
            "p (c t k b) -> p c t k b", c=CHUNKS, t=SC, k=2)
        pos = sb("pos", [P, CHUNKS, SC, 2])
        posI = sb("posI", [P, CHUNKS, SC, 2], I32)
        trash = sb("trash", [P, 2, NBLK])
        BATCHES = [(0, 1), (2, 3, 4)]
        NB = len(BATCHES)
        assert sum(map(len, BATCHES)) == SC
        rowB = sb("rowB", [P, CHUNKS, SC, RB])
        rec_area = sb("rec_area", [P, NPART * PT * RA])
        rowA = rec_area[:, 0:CHUNKS * SC * RA].rearrange("p (c t w) -> p c t w", c=CHUNKS, t=SC)
        rec = rec_area[:, :].rearrange("p (q t w) -> p q t w", q=NPART, t=PT)
        recB = sb("recB", [P, NPART, PT, RB])
        gat = sb("gat", [P, NPART, PT, 2 * F])
        oh = ring[:, 0:4 * PIECE].rearrange("p (r t n) -> p r t n", r=4, t=PT)
        ohT = ring[:, 4 * PIECE:5 * PIECE].rearrange("p (t n) -> p t n", t=PT)
        mask, scores, probs = oh[:, 0, :, :], ohT, oh[:, 1, :, :]
        nscore = ring[:, 2 * PIECE:4 * PIECE].rearrange("p (r n) -> p r n", r=2)
        nodes = sb("nodes", [P, NBLK, 2])
        pair = sb("pair", [P, PG, 2])
        other = sb("other", [P, PG, PG])
        cand = sb("cand", [P, PG, PG])
        gmax = sb("gmax", [P, PG])
        glow = sb("glow", [P, PG])
        lowest = sb("lowest", [P, PG])
        fall = sb("fall", [P, PG])
        fac = sb("fac", [P, 2, PG])
        work = sb("work", [P, 3 * PT * F])
        msg = work[:, 0:2 * PT * F].rearrange("p (r t f) -> p r t f", r=2, t=PT)
        msg2 = work[:, 2 * PT * F:3 * PT * F].rearrange("p (t f) -> p t f", t=PT)
        alpha = sb("alpha", [P, PT, HEADS])
        two = sb("two", [P, 2 * F])
        hT = sb("hT", [P, 2 * F])

        products = work[:, 0:SC * 2 * NBLK].rearrange("p (t k b) -> p t k b", t=SC, k=2)
        count_b = work[:, 0:NBLK]
        shift = work[:, NBLK:2 * NBLK]
        row_l = work[:, 2 * NBLK:2 * NBLK + NG // P]
        row_s = work[:, 2 * NBLK + NG // P:2 * NBLK + 2 * (NG // P)]

        bank = [ctx.enter_context(nc.psum_tensor(f"bank{b}", [P, 512], F32)) for b in range(8)]

        def sems(name, n):
            return [sem(f"{name}{k}") for k in range(n)]

        s_iota = sem("s_iota")
        s_in = sem("s_in")
        s_xin = sem("s_xin")
        s_x0 = sem("s_x0")
        s_win = sem("s_win")
        s_w0 = sem("s_w0")
        s_const = sem("s_const")
        s_ends = sem("s_ends")
        s_endsout = sem("s_endsout")
        s_unsorted = sem("s_unsorted")
        s_sorted = sem("s_sorted")
        s_order = sem("s_order")
        s_name = sem("s_name")
        s_fillsrc = sem("s_fillsrc")
        s_fill = sem("s_fill")
        s_dve = sem("s_dve")
        s_ckey = sems("s_ckey", CHUNKS)
        s_cnt = sems("s_cnt", CHUNKS)
        s_start = sem("s_start")
        s_blki = sem("s_blki")
        s_blk = sem("s_blk")
        s_skey = sems("s_skey", CHUNKS)
        s_rank = sem("s_rank")
        s_read = sem("s_read")
        s_chunk = sems("s_chunk", CHUNKS)
        s_rows = sems("s_rows", CHUNKS)
        s_wld = sems("s_wld", CHUNKS)
        s_posf = sem("s_posf")
        s_pos = sems("s_pos", CHUNKS)
        s_go = sem("s_go")
        s_scA = sems("s_scA", CHUNKS)
        s_scB = sems("s_scB", CHUNKS)
        s_rec = sems("s_rec", NPART)
        s_gat = [sems("s_gat_early", NPART), sems("s_gat_late", NPART)]
        s_var = sem("s_var")
        s_root = sem("s_root")
        s_y = sem("s_y")
        s_tab = sem("s_tab")
        s_oh = sem("s_oh")
        s_agg = sem("s_agg")
        s_acc = sem("s_acc")
        s_msk = sem("s_msk")
        s_zt = sem("s_zt")
        s_pair = sem("s_pair")
        s_t = sem("s_t")
        s_l = sem("s_l")
        s_low = sem("s_low")
        s_p = sem("s_p")
        s_pt = sem("s_pt")
        s_ptc = sem("s_ptc")
        s_oT = sem("s_oT")
        s_oTc = sem("s_oTc")
        s_qg = sem("s_qg")
        s_m = sem("s_m")
        s_msg = sem("s_msg")
        s_two = sem("s_two")
        s_tr = sem("s_tr")
        s_trc = sem("s_trc")
        s_pr = sem("s_pr")
        s_prc = sem("s_prc")
        s_accd = sem("s_accd")
        s_out = sem("s_out")

        block = ctx.enter_context(nc.Block())

        PASSES = ["B", "A", "B", "B", "B", "A"]
        LAST = len(PASSES) - 1
        NPP = ITERS * NPART
        LOADS = [16 * (PG if kind == "B" else JT if l == 1 else 1) for l, kind in enumerate(PASSES)]
        LOADED = [sum(LOADS[:l]) * ITERS for l in range(len(PASSES))]
        fileA_v = fileA.rearrange("(g p j) c -> p g j c", p=P, j=JT)

        def turns(eng, count, body, first=1, last=0):
            for i in range(first):
                body(i)
            with eng.Fori(first, count - last) as i:
                body(i)
            for i in range(count - last, count):
                body(i)

        def isfirst(i):
            return isinstance(i, int) and i == 0

        def part_before(i, q, k):
            return (i, q - k) if q >= k else None if isfirst(i) else (i - 1, q - k + NPART)

        def part_after(i, q, k):
            last = isinstance(i, int) and i == ITERS - 1
            return (i, q + k) if q + k < NPART else None if last else (i + 1, q + k - NPART)

        def node_rows(t):
            return t.rearrange("(b p) f -> p b f", p=P)

        @block.sync
        def _(sp):
            sp.dma_start(srcI, src.rearrange("(p t) -> p t", p=P)).then_inc(s_in, 16)
            sp.dma_start(dstI, dst.rearrange("(p t) -> p t", p=P)).then_inc(s_in, 16)
            sp.dma_start(phi, edge_weight.rearrange("(p t) -> p t", p=P)).then_inc(s_in, 16)
            sp.dma_start(phi2, edge_weight2.rearrange("(p t) -> p t", p=P)).then_inc(s_in, 16)
            sp.dma_start(wcols[:, 0, :], w_i.partition_broadcast(P)).then_inc(s_in, 16)
            sp.dma_start(wcols[:, 1, :], w_j.partition_broadcast(P)).then_inc(s_in, 16)
            sp.dma_start(next_i[0:P - 1, :], dst[T:E].rearrange("(p t) -> p t", t=T)[:, 0:1],
                         allow_slow_non_contiguous=True).then_inc(s_in, 16)
            sp.dma_start(next_i[P - 1:P, :], dst[E - 1:E].unsqueeze(0)).then_inc(s_in, 16)
            sp.wait_ge(s_fillsrc, 1)
            fA = fileA.rearrange("(k p r) c -> k p r c", p=P, r=FILL)
            fB = fileB[0:SLOTS, :].rearrange("(k p r) c -> k p r c", p=P, r=FILL)
            for k in range(SLOTS // (P * FILL)):
                sp.dma_start(fA[k], fillA).then_inc(s_fill, 16)
                sp.dma_start(fB[k], fillB).then_inc(s_fill, 16)
            sp.dma_start(fileB[SLOTS + E:SLOTS + E + GROUP, :].rearrange("(p r) c -> p r c", p=P), fillB[:, 0:JT, :]).then_inc(s_endsout, 16)
            sp.wait_ge(s_ends, 1)
            sp.dma_start(fileB[SLOTS:SLOTS + E, :].rearrange("(p t) c -> p t c", p=P), ends).then_inc(s_endsout, 16)
            sp.wait_ge(s_w0, 1)
            for b in range(2):
                for hd in range(HEADS):
                    rows = slice(b * F + hd * D, b * F + hd * D + D)
                    cols = slice(hd * D, hd * D + D)
                    sp.dma_start(Wqk[rows, b, 0, cols], Wq[hd]).then_inc(s_win, 16)
                    sp.dma_start(Wqk[rows, b, 1, cols], Wk[hd]).then_inc(s_win, 16)
                    sp.dma_start(Wvb[rows, b, cols], Wv[hd]).then_inc(s_win, 16)
            ea = edge_attr.rearrange("(p t) f -> p t f", p=P)
            def load_chunks(i):
                for c in range(CHUNKS):
                    if not isfirst(i):
                        sp.wait_ge(s_scA[c], i * (SC * 16))
                    sp.dma_start(rowA[:, c, :, 0:F], ea[:, bass.ds(i * (SC * CHUNKS) + c * SC, SC), :]).then_inc(s_wld[c], 16)

            turns(sp, TURNS, load_chunks)
            for c in range(CHUNKS):
                sp.wait_ge(s_scA[c], TURNS * SC * 16)
                sp.wait_ge(s_scB[c], TURNS * SC * 16)
            sp.wait_ge(s_blki, 1)
            for k in range(3):
                sp.dma_start(blkfile[k:k + 1, :].rearrange("o (p j) -> (o p) j", p=P), blk_i[:, k, :]).then_inc(s_blk, 16)
            sp.wait_ge(s_blk, 3 * 16)
            sp.wait_ge(s_endsout, 32)
            sp.wait_ge(s_x0, 1)
            sp.dma_start(rowrow, blkfile[2:3, :]).then_inc(s_blk, 16)
            sp.dma_start(node0.bitcast(I32), blkfile[1, :].partition_broadcast(P)).then_inc(s_blk, 16)
            sp.dma_start(blkrow[:, :, :], blkfile[0:2, :].unsqueeze(0)).then_inc(s_blk, 16)
            sp.wait_ge(s_x0, 1)
            sp.dma_start(x_sb[:, 0:NBLK - 1, :], node_rows(x[0:(NBLK - 1) * P, :])).then_inc(s_xin, 16)
            sp.dma_start(x_sb[0:REST, NBLK - 1, :], x[(NBLK - 1) * P:N, :]).then_inc(s_xin, 16)

            sp.wait_ge(s_blk, 6 * 16)
            rowreg = [sp.alloc_register(f"row{k}") for k in range(PG)]
            for l, kind in enumerate(PASSES):
                sp.wait_ge(s_y, l + 1)
                tv = node_rows(table[l])
                if l == 0:
                    half = NBLK // 2
                    sp.dma_start(tv[:, 0:half, :], hs[:, 0:half, :]).then_inc(s_tab, 16)
                    sp.dma_start(tv[:, half:NBLK, :], hs[:, half:NBLK, :]).then_inc(s_tab, 16)
                elif l == LAST:
                    sp.dma_start(tv[:, :, 0:F], tmp).then_inc(s_tab, 16)
                    sp.dma_start(tv[:, :, F:2 * F], h_sb).then_inc(s_tab, 16)
                else:
                    sp.dma_start(tv[:, :, 0:F // 2], tmp[:, :, 0:F // 2]).then_inc(s_tab, 16)
                    sp.dma_start(tv[:, :, F // 2:F], tmp[:, :, F // 2:F]).then_inc(s_tab, 16)

                def load_parts(i):
                    for q in range(NPART):
                        if l > 0 or not isfirst(i):
                            sp.wait_ge(s_agg, i * NPART + (l * NPP + q + 1 - NPART))
                        g = i * (NPART * PG) + q * PG
                        if kind == "B":
                            sp.load(rowreg, rowrow[:, bass.ds(g, PG)])
                            for k in range(PG):
                                row = sp.snap(rowreg[k], min_val=0, max_val=SLOTS + E)
                                sp.dma_start(recB[:, q, JT * k:JT * k + JT, :].rearrange("p j c -> p (j c)"),
                                             fileB[bass.ds(row, GROUP), :].rearrange("(p j) c -> p (j c)", j=JT)).then_inc(s_rec[q], 16)
                        elif l == LAST:
                            sp.dma_start(rec[:, q, :, :].rearrange("p (g j) c -> p g (j c)", j=JT),
                                         fileA_v[:, bass.ds(g, PG), :, :].rearrange("p g j c -> p g (j c)")).then_inc(s_rec[q], 16)
                        else:
                            for j in range(JT):
                                sp.dma_start(rec[:, q, :, F:RA].rearrange("p (g j) c -> p g j c", j=JT)[:, :, j, :],
                                             fileA_v[:, bass.ds(g, PG), j, F:RA]).then_inc(s_rec[q], 16)

                turns(sp, ITERS, load_parts, first=int(l == 0))
            sp.wait_ge(s_y, LAST + 2)
            sp.dma_start(node_rows(out[0:(NBLK - 1) * P, :]), x_sb[:, 0:NBLK - 1, :]).then_inc(s_out, 16)
            sp.dma_start(out[(NBLK - 1) * P:N, :], x_sb[0:REST, NBLK - 1, :]).then_inc(s_out, 16)
            sp.wait_ge(s_out, 32)

        @block.gpsimd
        def _(pool):
            nc.gpsimd.iota(iota_i[:, :], [[1, P]], base=0, channel_multiplier=0).then_inc(s_iota, 1)
            nc.gpsimd.iota(part_i[:, :], [[0, 1]], base=0, channel_multiplier=1).then_inc(s_iota, 1)
            nc.gpsimd.iota(gnum_i[:, :], [[1, NG // P]], base=0, channel_multiplier=NG // P).then_inc(s_iota, 1)
            pool.wait_ge(s_fill, 2 * 16 * (SLOTS // (P * FILL)))
            pool.wait_ge(s_order, 1)

            def rows_out(into_b):
                with pool.Fori(0, TURNS) as i:
                    for c in range(CHUNKS):
                        pool.wait_ge(s_wld[c], i * 16 + 16)
                        pool.wait_ge(s_rows[c], i + 1)
                        pool.wait_ge(s_pos[c], i + 1)
                        pool.sem_inc(s_go, 1)
                        for t in range(SC):
                            pool.indirect_dma_start(fileA, bass.IndirectOffsetOnAxis(ap=posI[:, c, t, 0:1], axis=0),
                                                    rowA[:, c, t, :], None).then_inc(s_scA[c], 16)
                            if into_b:
                                pool.indirect_dma_start(fileB, bass.IndirectOffsetOnAxis(ap=posI[:, c, t, 1:2], axis=0),
                                                        rowB[:, c, t, :], None).then_inc(s_scB[c], 16)
                        if not into_b:
                            pool.sem_inc(s_scB[c], SC * 16)

            order = pool.alloc_register("order")
            pool.load(order, in_order_i[0:1, 0:1])
            with pool.If_eq(order, 0):
                rows_out(True)
            with pool.Else():
                rows_out(False)
            for l, kind in enumerate(PASSES):
                index = recB[:, :, :, 1:2] if kind == "B" else rec[:, :, :, A_IDX:A_IDX + 1]
                pool.wait_ge(s_tab, 32 * (l + 1))
                with pool.Fori(0, ITERS) as i:
                    for q in range(NPART):
                        pool.wait_ge(s_rec[q], i * LOADS[l] + (LOADED[l] + LOADS[l]))
                        pool.sem_inc(s_go, 1)
                        for t in range(PT):
                            pool.indirect_dma_start(gat[:, q, t, 0:TABW[l]], None, table[l], bass.IndirectOffsetOnAxis(
                                ap=index[:, q, t, :].bitcast(I32), axis=0)).then_inc(s_gat[l // 3][q], 16)

        @block.tensor
        def _(pe):
            cnt = [bank[0], bank[1]]
            ranks = [bank[2], bank[5], bank[6]]
            deg = [bank[3], bank[4]]
            pe.wait_ge(s_const, 1)
            for k in range(2):
                nc.tensor.matmul(cnt[k][:, 0:SC * NBLK], ones_b[:, :], zeros_b[:, 0:SC * NBLK],
                                 start=True, stop=False, skip_group_check=True)
            pe.wait_ge(s_unsorted, 1)
            nc.tensor.matmul(bank[7][:, 0:1], ones_b[:, :], unsorted[:, :], start=True, stop=True).then_inc(s_sorted, 1)
            with pe.Fori(0, TURNS) as i:
                for c in range(CHUNKS):
                    pe.wait_ge(s_ckey[c], i + 1)
                    for k in range(2):
                        mm = nc.tensor.matmul(cnt[k][:, 0:SC * NBLK], ones_b[:, :], ohkey[:, c, :, k, :],
                                              start=False, stop=False, skip_group_check=True)
                    mm.then_inc(s_cnt[c], 1)
            pe.wait_ge(s_start, 1)
            for rank in ranks:
                nc.tensor.matmul(rank[:, 0:2 * NBLK], ident[:, :], start_rows, start=True, stop=False, skip_group_check=True)
            for k in range(2):
                nc.tensor.matmul(deg[k][:, 0:NBLK], ones_b[:, :], zeros_b[:, 0:NBLK],
                                 start=True, stop=False, skip_group_check=True)

            def advance(rank, by, c, t):
                return nc.tensor.matmul(rank[:, 0:2 * NBLK], by[:, :], ohkey[:, c, t, :, :].rearrange("p k b -> p (k b)"),
                                        start=False, stop=False, skip_group_check=True)

            with pe.Fori(0, TURNS) as i:
                for c in range(CHUNKS):
                    pe.wait_ge(s_skey[c], i + 1)
                    for n, tiles in enumerate(BATCHES):
                        for j, t in enumerate(tiles):
                            for t0 in tiles[:j]:
                                advance(ranks[j], ones_b, c, t0)
                            mm = advance(ranks[j], before, c, t)
                        mm.then_inc(s_rank, 1)
                        for t in tiles:
                            for k in range(2):
                                nc.tensor.matmul(deg[k][:, 0:NBLK], ohlo[:, c, t, k, :], ohkey[:, c, t, k, :],
                                                 start=False, stop=False, skip_group_check=True)
                        pe.wait_ge(s_read, i * (CHUNKS * NB) + (c * NB + n + 1))
                        for j, rank in enumerate(ranks):
                            if j < len(tiles):
                                mm = advance(rank, upto, c, tiles[j])
                            for t0 in tiles[j + 1:] if j < len(tiles) else tiles:
                                mm = advance(rank, ones_b, c, t0)
                    mm.then_inc(s_chunk[c], 1)

            def sums(l, i, q, left, right, width=F):
                for t in range(PT):
                    k = t // JT
                    mm = nc.tensor.matmul(bank[4 + q % 2][:, k * width:k * width + width], left[:, t, :], right[:, t, 0:width],
                                          start=(t % JT == 0), stop=(t % JT == JT - 1))
                mm.then_inc(s_agg, 1)

            def weighted_sums(i, q):
                pe.wait_ge(s_ptc, i * NPART + q + 1)
                sums(0, i, q, probs, gat[:, q, :, :], F + 1)

            def exponentials_back(i, q):
                pe.wait_ge(s_p, i * NPART + q + 1)
                for t in range(PT):
                    mm = nc.tensor.transpose(bank[2 + t // 4][:, t % 4 * P:t % 4 * P + P],
                                             nscore[:, q % 2, t * P:t * P + P], ident[:, :])
                mm.then_inc(s_pt, 1)

            def attend(i):
                for q in range(NPART):
                    if part_before(i, q, 2):
                        weighted_sums(*part_before(i, q, 2))
                    pe.wait_ge(s_msk, i * NPART + q + 1)
                    for t in range(PT):
                        mm = nc.tensor.transpose(bank[t // 4][:, t % 4 * P:t % 4 * P + P], scores[:, t, :], ident[:, :])
                    mm.then_inc(s_zt, 1)
                    if part_before(i, q, 1):
                        exponentials_back(*part_before(i, q, 1))

            turns(pe, ITERS, attend)
            weighted_sums(ITERS - 1, NPART - 2)
            exponentials_back(ITERS - 1, NPART - 1)
            weighted_sums(ITERS - 1, NPART - 1)
            for l in range(1, LAST):
                with pe.Fori(0, ITERS) as i:
                    for q in range(NPART):
                        pe.wait_ge(s_oh, i * NPART + (l * NPP + q + 1))
                        pe.wait_ge(s_gat[l // 3][q], i * (16 * PT) + (l % 3 * ITERS + 1) * 16 * PT)
                        sums(l, i, q, oh[:, q, :, :], gat[:, q, :, :])

            def project(weights, width, n0):
                def pair(i):
                    pe.wait_ge(s_two, i + (n0 + 1))
                    nc.tensor.transpose(bank[0][:, 0:P], two[:, :], ident[:, :]).then_inc(s_tr, 1)
                    pe.wait_ge(s_trc, i + (n0 + 1))
                    if n0 > 0 or not isfirst(i):
                        pe.wait_ge(s_prc, i + n0)
                    nc.tensor.matmul(bank[1][:, 0:width], hT[:, :], weights, start=True, stop=True).then_inc(s_pr, 1)

                turns(pe, NBLK // 2, pair)

            pe.wait_ge(s_win, 24 * 16)
            project(Wqk[:, :, :, :].rearrange("p b k f -> p (b k f)"), 4 * F, 0)
            pe.wait_ge(s_prc, NBLK // 2)
            breg = [pe.alloc_register(f"block{k}") for k in range(PG)]

            def ones_back(i, q):
                pe.wait_ge(s_oh, i * NPART + (LAST * NPP + q + 1))
                for t in range(PT):
                    mm = nc.tensor.transpose(bank[t // 4][:, t % 4 * P:t % 4 * P + P], oh[:, q, t, :], ident[:, :])
                mm.then_inc(s_oT, 1)

            def edge_queries(i, q):
                n = i * NPART + q
                pe.load(breg, blkrow[0:1, 0, bass.ds(i * (NPART * PG) + q * PG, PG)])
                blocks = [pe.snap(r, min_val=0, max_val=NBLK - 1) for r in breg]
                pe.wait_ge(s_oTc, n + 1)
                for t in range(PT):
                    mm = nc.tensor.matmul(bank[2][:, t * F:t * F + F], ohT[:, t, :],
                                          q_sb[:, bass.ds(blocks[t // JT], 1), :].rearrange("p b f -> p (b f)"),
                                          start=True, stop=True)
                mm.then_inc(s_qg, 1)

            def pairs(i):
                for q in range(NPART):
                    new, old = part_after(i, q, 1), part_before(i, q, 1)
                    if new:
                        ones_back(*new)
                    if old:
                        sums(LAST, *old, oh[:, old[1], :, :], msg[:, old[1] % 2, :, :])
                    pe.wait_ge(s_msg, i * NPART + q + 1)
                    if new:
                        edge_queries(*new)

            ones_back(0, 0)
            edge_queries(0, 0)
            turns(pe, ITERS, pairs, first=1, last=1)
            sums(LAST, ITERS - 1, NPART - 1, oh[:, NPART - 1, :, :], msg[:, (NPART - 1) % 2, :, :])
            project(Wvb[:, :, :].rearrange("p b f -> p (b f)"), 2 * F, NBLK // 2)

        @block.scalar
        def _(act):
            act.wait_ge(s_const, 1)
            def put_together(i):
                for c in range(CHUNKS):
                    if not isfirst(i):
                        act.wait_ge(s_scA[c], i * (SC * 16))
                        act.wait_ge(s_scB[c], i * (SC * 16))
                    cols = bass.ds(i * (SC * CHUNKS) + c * SC, SC)
                    nc.scalar.copy(rowA[:, c, :, A_LO], los[:, 2, cols])
                    nc.scalar.copy(rowA[:, c, :, A_LON], los[:, 0, cols])
                    nc.scalar.copy(rowA[:, c, :, A_PHI], phi[:, cols])
                    nc.scalar.copy(rowA[:, c, :, A_IDX].bitcast(I32), dstI[:, cols])
                    nc.scalar.copy(rowB[:, c, :, 0], dstI[:, cols])
                    nc.scalar.copy(rowB[:, c, :, 1].bitcast(I32), srcI[:, cols]).then_inc(s_rows[c], 1)

            turns(act, TURNS, put_together)

            def root(n, rows):
                act.wait_ge(s_var, n)
                nc.scalar.activation(stat[:, rows, :], stat[:, rows, :], ACT.Sqrt).then_inc(s_root, 1)

            root(1, slice(0, 2))
            root(2, slice(1, 2))
            def exponentials(i, q):
                act.wait_ge(s_l, i * NPART + q + 1)
                nc.scalar.activation(fac[:, q % 2, :], fall[:, :], ACT.Exp)
                for k in range(PG):
                    g = nscore[:, q % 2, k * GROUP:k * GROUP + GROUP]
                    a = nc.scalar.activation(g, g, ACT.Exp, bias=lowest[:, k:k + 1])
                a.then_inc(s_p, 1)

            def exponentials_out(i, q, first=False):
                n = i * NPART + q
                act.wait_ge(s_pt, n + 1)
                if not first:
                    act.wait_ge(s_agg, n)
                for r in range(2):
                    a = nc.scalar.copy(probs[:, 4 * r:4 * r + 4, :].rearrange("p t n -> p (t n)"), bank[2 + r][:, :])
                a.then_inc(s_ptc, 1)

            def attend(i):
                for q in range(NPART):
                    n = i * NPART + q
                    if part_before(i, q, 2):
                        exponentials_out(*part_before(i, q, 2), first=isfirst(i) and q == 2)
                    act.wait_ge(s_oh, n + 1)
                    if part_before(i, q, 1):
                        act.wait_ge(s_zt, n)
                    act.wait_ge(s_gat[0][q], i * (16 * PT) + 16 * PT)
                    for t in range(PT):
                        a = nc.scalar.activation(scores[:, t, :], mask[:, t, :], ACT.Identity,
                                                 bias=gat[:, q, t, F + 1:F + 2], scale=-HUGE)
                    a.then_inc(s_msk, 1)
                    if part_before(i, q, 1):
                        exponentials(*part_before(i, q, 1))
                    act.wait_ge(s_zt, n + 1)
                    act.wait_ge(s_pair, n + 1)
                    for k in range(PG):
                        a = nc.scalar.activation(nscore[:, q % 2, k * GROUP:k * GROUP + GROUP],
                                                 bank[k // 2][:, k % 2 * GROUP:k % 2 * GROUP + GROUP],
                                                 ACT.Identity, bias=pair[:, k, 0:1])
                    a.then_inc(s_t, 1)

            turns(act, ITERS, attend)
            exponentials_out(ITERS - 1, NPART - 2)
            exponentials(ITERS - 1, NPART - 1)
            exponentials_out(ITERS - 1, NPART - 1)

            def project(source, n0):
                def pair(i):
                    nc.scalar.copy(two[:, :].rearrange("p (b f) -> p b f", b=2),
                                   source[:, bass.ds(i * 2, 2), :]).then_inc(s_two, 1)
                    act.wait_ge(s_tr, i + (n0 + 1))
                    if n0 > 0 or not isfirst(i):
                        act.wait_ge(s_pr, i + n0)
                    nc.scalar.copy(hT[:, :], bank[0][:, 0:P]).then_inc(s_trc, 1)

                turns(act, NBLK // 2, pair)

            root(3, slice(1, 2))
            root(4, slice(1, 2))
            root(5, slice(1, 2))
            act.wait_ge(s_m, 1)
            project(h_sb, 0)

            def ones_out(i):
                for q in range(NPART):
                    n = i * NPART + q
                    act.wait_ge(s_oT, n + 1)
                    if not (isfirst(i) and q == 0):
                        act.wait_ge(s_qg, n)
                    for b in range(2):
                        a = nc.scalar.copy(ohT[:, 4 * b:4 * b + 4, :].rearrange("p t n -> p (t n)"), bank[b][:, :])
                    a.then_inc(s_oTc, 1)

            turns(act, ITERS, ones_out)
            act.wait_ge(s_accd, 1)
            project(acc, NBLK // 2)

        @block.vector
        def _(v):
            done = [0]

            def nth():
                done[0] += 1
                return done[0]

            v.wait_ge(s_iota, 3)
            nc.vector.tensor_copy(iota[:, :], iota_i[:, :]).then_inc(s_dve, 1)
            v.wait_ge(s_dve, nth())
            nc.vector.tensor_copy(part[:, :], part_i[:, :]).then_inc(s_dve, 1)
            v.wait_ge(s_dve, nth())
            nc.vector.tensor_copy(gnum[:, :], gnum_i[:, :])
            nc.vector.tensor_copy(iota_b[:, :], iota_i[:, :])
            nc.vector.tensor_scalar(ident[:, :], iota[:, :], part[:, 0:1], None, ALU.is_equal)
            nc.vector.tensor_scalar(before[:, :], iota[:, :], part[:, 0:1], None, ALU.is_gt)
            nc.vector.tensor_scalar(upto[:, :], iota[:, :], part[:, 0:1], None, ALU.is_le)
            nc.vector.memset(ones_b[:, :], 1.0)
            nc.vector.memset(zeros_b[:, :], 0.0)
            nc.vector.memset(Wqk[:, :, :, :], 0.0)
            nc.vector.memset(Wvb[:, :, :], 0.0).then_inc(s_w0, 1)
            nc.vector.memset(fillA[:, :, :], 0.0)
            nc.vector.memset(fillB[:, :, :], 0.0).then_inc(s_dve, 1)
            v.wait_ge(s_dve, nth())
            nc.vector.memset(fillA[:, :, A_LO:A_LON + 1], -1.0)
            nc.vector.memset(fillB[:, :, 0:1], -1.0).then_inc(s_fillsrc, 1)
            v.wait_ge(s_in, 8 * 16)
            for k, end in enumerate((srcI, dstI)):
                nc.vector.tensor_single_scalar(work_i, end, 7, ALU.arith_shift_right).then_inc(s_dve, 1)
                v.wait_ge(s_dve, nth())
                nc.vector.tensor_copy(keys[:, k, 0:T], work_i).then_inc(s_dve, 1)
                v.wait_ge(s_dve, nth())
                nc.vector.tensor_single_scalar(work_i, end, P - 1, ALU.bitwise_and).then_inc(s_dve, 1)
                v.wait_ge(s_dve, nth())
                nc.vector.tensor_copy(los[:, 2 - k, 0:T], work_i).then_inc(s_dve, 1)
                v.wait_ge(s_dve, nth())
            nc.vector.tensor_tensor(phi, phi, phi2, ALU.mult)
            nc.vector.tensor_tensor(work_i.bitcast(F32), srcI, dstI, ALU.not_equal)
            nc.vector.tensor_scalar(los[:, 0, 0:T], los[:, 2, 0:T], 1.0, None, ALU.add).then_inc(s_dve, 1)
            v.wait_ge(s_dve, nth())
            nc.vector.tensor_tensor(los[:, 0, 0:T], los[:, 0, 0:T], work_i.bitcast(F32), ALU.mult).then_inc(s_dve, 1)
            v.wait_ge(s_dve, nth())
            nc.vector.tensor_scalar(los[:, 0, 0:T], los[:, 0, 0:T], -1.0, None, ALU.add).then_inc(s_const, 1)
            v.wait_ge(s_const, 1)
            nc.vector.tensor_copy(ends[:, :, 0], dstI)
            nc.vector.tensor_copy(next_f[:, :], next_i[:, :])
            nc.vector.tensor_copy(ends[:, :, 1].bitcast(I32), srcI).then_inc(s_ends, 1)
            v.wait_ge(s_ends, 1)
            nc.vector.tensor_tensor(ring[:, 0:T - 1], ends[:, 0:T - 1, 0], ends[:, 1:T, 0], ALU.is_le)
            nc.vector.tensor_tensor(ring[:, T - 1:T], ends[:, T - 1:T, 0], next_f[:, :], ALU.is_le).then_inc(s_dve, 1)
            v.wait_ge(s_dve, nth())
            nc.vector.tensor_reduce(rising[:, :], ring[:, 0:T], AX.X, ALU.add).then_inc(s_dve, 1)
            v.wait_ge(s_dve, nth())
            nc.vector.tensor_scalar(unsorted[:, :], rising[:, :], float(T), None, ALU.is_lt).then_inc(s_unsorted, 1)

            def ones_by_block(c, i):
                cols = bass.ds(i * (SC * CHUNKS) + c * SC, SC)
                for k in range(2):
                    last = nc.vector.tensor_tensor(
                        ohkey[:, c, :, k, :], iota_b[:, 0:NBLK].unsqueeze(1).broadcast_to((P, SC, NBLK)),
                        keys[:, k, cols].unsqueeze(2).broadcast_to((P, SC, NBLK)), ALU.is_equal)
                return last

            def count(i):
                for c in range(CHUNKS):
                    if not isfirst(i):
                        v.wait_ge(s_cnt[c], i)
                    ones_by_block(c, i).then_inc(s_ckey[c], 1)

            turns(v, TURNS, count)
            for c in range(CHUNKS):
                v.wait_ge(s_cnt[c], TURNS)
            for k in range(2):
                nc.vector.tensor_reduce(cntf[:, k, :], bank[k][:, 0:SC * NBLK].rearrange("p (t b) -> p b t", t=SC),
                                        AX.X, ALU.add).then_inc(s_dve, 1)
                v.wait_ge(s_dve, nth())
            v.wait_ge(s_sorted, 1)
            nc.vector.tensor_scalar(in_order[:, :], bank[7][:, 0:1], 0.0, None, ALU.is_equal)
            nc.vector.tensor_copy(count_b, cntf[:, 1, :]).then_inc(s_dve, 1)
            v.wait_ge(s_dve, nth())
            nc.vector.tensor_copy(in_order_i[:, :], in_order[:, :]).then_inc(s_order, 1)
            nc.vector.tensor_scalar(cnti[:, :, :], cntf[:, :, :], float(GROUP - 1), None, ALU.add).then_inc(s_dve, 1)
            v.wait_ge(s_dve, nth())
            nc.vector.tensor_single_scalar(cnti[:, :, :], cnti[:, :, :], GROUP.bit_length() - 1,
                                           ALU.arith_shift_right).then_inc(s_dve, 1)
            v.wait_ge(s_dve, nth())
            nc.vector.tensor_copy(cntf[:, :, :], cnti[:, :, :]).then_inc(s_dve, 1)
            v.wait_ge(s_dve, nth())
            for k in range(2):
                nc.vector.tensor_tensor_scan(start[:, k, :], cntf[:, k, :], zeros_b[:, 0:NBLK], 0.0, ALU.add, ALU.add).then_inc(s_dve, 1)
                v.wait_ge(s_dve, nth())
            nc.vector.tensor_tensor(start[:, :, :], start[:, :, :], cntf[:, :, :], ALU.subtract).then_inc(s_dve, 1)
            v.wait_ge(s_dve, nth())
            nc.vector.tensor_scalar(start_rows, start[:, :, :].rearrange("p k b -> p (k b)"), float(GROUP), None,
                                    ALU.mult).then_inc(s_start, 1)
            nc.vector.memset(shift[:, 0:1], 0.0)
            nc.vector.scalar_tensor_tensor(shift[:, 1:NBLK], cntf[:, 1, 0:NBLK - 1], -float(GROUP), count_b[:, 0:NBLK - 1],
                                           ALU.mult, ALU.add).then_inc(s_dve, 1)
            v.wait_ge(s_dve, nth())
            GC = NG // P
            for k in range(2):
                cmp = ring[:, 0:GC * NBLK].rearrange("p (g b) -> p g b", b=NBLK)
                nc.vector.tensor_tensor(cmp, start[:, k, :].unsqueeze(1).broadcast_to((P, GC, NBLK)),
                                        gnum[:, :].unsqueeze(2).broadcast_to((P, GC, NBLK)), ALU.is_le).then_inc(s_dve, 1)
                v.wait_ge(s_dve, nth())
                nc.vector.tensor_reduce(trash[:, 0, 0:GC], cmp, AX.X, ALU.add).then_inc(s_dve, 1)
                v.wait_ge(s_dve, nth())
                nc.vector.tensor_scalar(blk_i[:, k, :], trash[:, 0, 0:GC], -1.0, None, ALU.add).then_inc(s_dve, 1)
                v.wait_ge(s_dve, nth())
            nc.vector.tensor_tensor(cmp, cmp, shift.unsqueeze(1).broadcast_to((P, GC, NBLK)), ALU.mult)
            nc.vector.tensor_scalar(row_l, gnum[:, :], float(GROUP), None, ALU.mult).then_inc(s_dve, 1)
            v.wait_ge(s_dve, nth())
            nc.vector.tensor_reduce(row_s, cmp, AX.X, ALU.add).then_inc(s_dve, 1)
            v.wait_ge(s_dve, nth())
            nc.vector.tensor_tensor(row_s, row_s, row_l, ALU.add).then_inc(s_dve, 1)
            v.wait_ge(s_dve, nth())
            nc.vector.tensor_scalar(row_s, row_s, float(E), float(SLOTS), ALU.min, ALU.add).then_inc(s_dve, 1)
            v.wait_ge(s_dve, nth())
            nc.vector.tensor_tensor(row_s, row_s, row_l, ALU.subtract).then_inc(s_dve, 1)
            v.wait_ge(s_dve, nth())
            nc.vector.scalar_tensor_tensor(row_s, row_s, in_order[:, 0:1], row_l, ALU.mult, ALU.add).then_inc(s_dve, 1)
            v.wait_ge(s_dve, nth())
            nc.vector.tensor_copy(blk_i[:, 2, :], row_s).then_inc(s_blki, 1)

            def chunk_after(i, c, k):
                last = isinstance(i, int) and i == TURNS - 1
                return (i, c + k) if c + k < CHUNKS else None if last else (i + 1, c + k - CHUNKS)

            def keys_of(i, c):
                if not isfirst(i):
                    v.wait_ge(s_chunk[c], i)
                ones_by_block(c, i)

            def nodes_of(i, c):
                cols = bass.ds(i * (SC * CHUNKS) + c * SC, SC)
                for k in range(2):
                    last = nc.vector.tensor_tensor(
                        ohlo[:, c, :, k, :], iota_b[:, :].unsqueeze(1).broadcast_to((P, SC, P)),
                        los[:, k, cols].unsqueeze(2).broadcast_to((P, SC, P)), ALU.is_equal)
                last.then_inc(s_skey[c], 1)

            def places(i, c, n):
                step = i * (CHUNKS * NB) + (c * NB + n + 1)
                v.wait_ge(s_rank, step)
                for j, t in enumerate(BATCHES[n]):
                    for k in range(2):
                        last = nc.vector.tensor_tensor_reduce(
                            products[:, t, k, :], ohkey[:, c, t, k, :], bank[(2, 5, 6)[j]][:, k * NBLK:k * NBLK + NBLK],
                            1.0, 0.0, ALU.mult, ALU.add, pos[:, c, t, k:k + 1])
                last.then_inc(s_read, 1)

            def sort(i):
                for c in range(CHUNKS):
                    new = chunk_after(i, c, 2)
                    v.wait_ge(s_skey[c], i + 1)
                    places(i, c, 0)
                    if new:
                        keys_of(*new)
                    places(i, c, 1)
                    if new:
                        nodes_of(*new)
                    v.wait_ge(s_read, i * (CHUNKS * NB) + (c * NB + NB))
                    if not isfirst(i):
                        v.wait_ge(s_scA[c], i * (SC * 16))
                        v.wait_ge(s_scB[c], i * (SC * 16))
                    nc.vector.tensor_copy(posI[:, c, :, :], pos[:, c, :, :]).then_inc(s_pos[c], 1)

            v.wait_ge(s_blki, 1)
            for c in range(2):
                keys_of(0, c)
                nodes_of(0, c)
            turns(v, TURNS, sort, last=1)
            for c in range(CHUNKS):
                v.wait_ge(s_chunk[c], TURNS)
            for k in range(2):
                nc.vector.tensor_copy(degs[:, k, :], bank[3 + k][:, 0:NBLK]).then_inc(s_dve, 1)
                v.wait_ge(s_dve, nth())
            nc.vector.tensor_scalar(stat[:, 0, :], degs[:, 0, :], 1.0, None, ALU.add)
            nc.vector.tensor_scalar(stat[:, 1, :], degs[:, 1, :], 1.0, None, ALU.max).then_inc(s_var, 1)
            v.wait_ge(s_root, 1)
            nc.vector.reciprocal(dinv1[:, :], stat[:, 0, :]).then_inc(s_dve, 1)
            v.wait_ge(s_dve, nth())
            nc.vector.reciprocal(dinv2[:, :], stat[:, 1, :]).then_inc(s_dve, 1)
            v.wait_ge(s_dve, nth())
            nc.vector.tensor_scalar(trash[:, 0, :], degs[:, 1, :], 0.0, None, ALU.is_gt).then_inc(s_dve, 1)
            v.wait_ge(s_dve, nth())
            nc.vector.tensor_tensor(dinv2[:, :], dinv2[:, :], trash[:, 0, :], ALU.mult).then_inc(s_dve, 1)
            v.wait_ge(s_dve, nth())
            for c in range(CHUNKS):
                v.wait_ge(s_scA[c], TURNS * SC * 16)
                v.wait_ge(s_scB[c], TURNS * SC * 16)
            nc.vector.memset(x_sb[:, NBLK - 1, :], 0.0).then_inc(s_x0, 1)
            v.wait_ge(s_xin, 32)

            def by_node(col):
                return col.unsqueeze(2).broadcast_to((P, NBLK, F))

            roots = [1]

            def layernorm():
                nc.vector.tensor_reduce(stat[:, 0, :], x_sb, AX.X, ALU.add).then_inc(s_dve, 1)
                v.wait_ge(s_dve, nth())
                nc.vector.tensor_scalar(stat[:, 0, :], stat[:, 0, :], -1.0 / F, None, ALU.mult).then_inc(s_dve, 1)
                v.wait_ge(s_dve, nth())
                nc.vector.tensor_tensor(tmp, x_sb, by_node(stat[:, 0, :]), ALU.add).then_inc(s_dve, 1)
                v.wait_ge(s_dve, nth())
                nc.vector.tensor_tensor(h_sb, tmp, tmp, ALU.mult).then_inc(s_dve, 1)
                v.wait_ge(s_dve, nth())
                nc.vector.tensor_reduce(stat[:, 1, :], h_sb, AX.X, ALU.add).then_inc(s_dve, 1)
                v.wait_ge(s_dve, nth())
                nc.vector.tensor_scalar(stat[:, 1, :], stat[:, 1, :], 1.0 / F, EPS, ALU.mult, ALU.add).then_inc(s_var, 1)
                roots[0] += 1
                v.wait_ge(s_root, roots[0])
                nc.vector.reciprocal(stat[:, 1, :], stat[:, 1, :]).then_inc(s_dve, 1)
                v.wait_ge(s_dve, nth())
                nc.vector.tensor_tensor(h_sb, tmp, by_node(stat[:, 1, :]), ALU.mult).then_inc(s_dve, 1)
                v.wait_ge(s_dve, nth())
                nc.vector.tensor_scalar(h_sb, h_sb, 0.0, None, ALU.max).then_inc(s_dve, 1)
                v.wait_ge(s_dve, nth())

            breg = [v.alloc_register(f"vblock{k}") for k in range(PG)]

            def load_blocks(kind, i, q):
                which = 0 if kind == "A" else 1
                v.load(breg, blkrow[0:1, which, bass.ds(i * (NPART * PG) + q * PG, PG)])
                return [v.snap(r, min_val=0, max_val=NBLK - 1) for r in breg]

            def ones_by_node(names, op, q):
                nc.vector.tensor_tensor(oh[:, q, :, :], iota[:, :].unsqueeze(1).broadcast_to((P, PT, P)),
                                        names.unsqueeze(2).broadcast_to((P, PT, P)), op).then_inc(s_oh, 1)

            v.wait_ge(s_blk, 6 * 16)
            layernorm()
            for k in range(2):
                nc.vector.tensor_tensor(tmp, h_sb, wcols[:, k, :].unsqueeze(1).broadcast_to((P, NBLK, F)), ALU.mult).then_inc(s_dve, 1)
                v.wait_ge(s_dve, nth())
                nc.vector.tensor_reduce(stat[:, k, :], tmp, AX.X, ALU.add).then_inc(s_dve, 1)
                v.wait_ge(s_dve, nth())
            nc.vector.tensor_copy(node0, node0.bitcast(I32)).then_inc(s_dve, 1)
            v.wait_ge(s_dve, nth())
            nc.vector.tensor_scalar(node0, node0, float(P), None, ALU.mult).then_inc(s_dve, 1)
            v.wait_ge(s_dve, nth())
            nc.vector.tensor_tensor(trash[:, 0, :], stat[:, 0, :], stat[:, 1, :], ALU.add).then_inc(s_dve, 1)
            v.wait_ge(s_dve, nth())
            nc.vector.scalar_tensor_tensor(trash[:, 1, :], trash[:, 0, :], 0.01, trash[:, 0, :], ALU.mult, ALU.max).then_inc(s_dve, 1)
            v.wait_ge(s_dve, nth())
            nc.vector.tensor_scalar(nodes[:, :, 1], trash[:, 1, :], -1.0, None, ALU.mult)
            nc.vector.tensor_copy(nodes[:, :, 0], stat[:, 0, :])
            nc.vector.memset(acc1[:, :, F:F + 1], 1.0)
            nc.vector.tensor_copy(acc1[:, :, 0:F], h_sb)
            nc.vector.memset(hs[:, :, F:F + 1], 1.0)
            nc.vector.tensor_copy(hs[:, :, F + 1], stat[:, 1, :])
            nc.vector.tensor_copy(hs[:, :, 0:F], h_sb).then_inc(s_dve, 1)
            v.wait_ge(s_dve, nth())
            v.sem_inc(s_y, 1)

            def name_targets(l, i, q):
                v.wait_ge(s_rec[q], i * LOADS[l] + (LOADED[l] + LOADS[l]))
                names = recB[:, q, :, 0].rearrange("p (g j) -> p g j", j=JT)
                first = node0[:, bass.ds(i * (NPART * PG) + q * PG, PG)]
                nc.vector.tensor_tensor(names, names, first.unsqueeze(2).broadcast_to((P, PG, JT)), ALU.subtract).then_inc(s_name, 1)
                v.wait_ge(s_name, i * NPART + (PASSES[:l].count("B") * NPP + q + 1))

            def masks(i, q):
                n = i * NPART + q
                name_targets(0, i, q)
                if not (isinstance(n, int) and n == 0):
                    v.wait_ge(s_msk, n)
                nc.vector.tensor_tensor(mask, iota[:, :].unsqueeze(1).broadcast_to((P, PT, P)),
                                        recB[:, q, :, 0].unsqueeze(2).broadcast_to((P, PT, P)), ALU.not_equal).then_inc(s_oh, 1)

            def maxima(i, q):
                n = i * NPART + q
                STEPS = 11
                g = i * (NPART * PG) + q * PG
                b = load_blocks("B", i, q)
                mine = node0[:, bass.ds(g, PG)]
                nc.vector.tensor_tensor(other[:, :, :], mine.unsqueeze(2).broadcast_to((P, PG, PG)),
                                        mine.unsqueeze(1).broadcast_to((P, PG, PG)), ALU.not_equal).then_inc(s_low, 1)
                v.wait_ge(s_t, n + 1)
                e = nscore[:, q % 2, :]
                nc.vector.scalar_tensor_tensor(e, e, 0.01, e, ALU.mult, ALU.max).then_inc(s_low, 1)
                v.wait_ge(s_low, n * STEPS + 2)
                nc.vector.tensor_reduce(gmax[:, :], e.rearrange("p (k e) -> p k e", k=PG), AX.X, ALU.max).then_inc(s_low, 1)
                v.wait_ge(s_low, n * STEPS + 3)
                nc.vector.scalar_tensor_tensor(cand[:, :, :], other[:, :, :], HUGE, gmax[:, :].unsqueeze(1).broadcast_to((P, PG, PG)),
                                               ALU.mult, ALU.subtract).then_inc(s_low, 1)
                v.wait_ge(s_low, n * STEPS + 4)
                nc.vector.tensor_reduce(glow[:, :], cand[:, :, :], AX.X, ALU.min).then_inc(s_low, 1)
                v.wait_ge(s_low, n * STEPS + 5)
                nc.vector.tensor_tensor(lowest[:, :], glow[:, :], pair[:, :, 1], ALU.min).then_inc(s_low, 1)
                v.wait_ge(s_low, n * STEPS + 6)
                nc.vector.tensor_tensor(fall[:, :], lowest[:, :], pair[:, :, 1], ALU.subtract).then_inc(s_low, 1)
                v.wait_ge(s_low, n * STEPS + 7)
                after_first = other[:, :, :].rearrange("p k j -> p (k j)")[:, PG:PG * PG:PG + 1]
                nc.vector.tensor_tensor(fall[:, 1:PG], fall[:, 1:PG], after_first, ALU.mult).then_inc(s_l, 1)
                for k in range(PG):
                    nc.vector.tensor_scalar(nodes[:, bass.ds(b[k], 1), 1], lowest[:, k:k + 1], 1.0, None, ALU.mult).then_inc(s_low, 1)
                    v.wait_ge(s_low, n * STEPS + (8 + k))

            def add_weighted(i, q):
                n = i * NPART + q
                b = load_blocks("B", i, q)
                v.wait_ge(s_agg, n + 1)
                W = F + 1
                for k in range(PG):
                    here = acc1[:, bass.ds(b[k], 1), :].rearrange("p b f -> p (b f)")
                    nc.vector.scalar_tensor_tensor(here, here, fac[:, q % 2, k:k + 1], bank[4 + q % 2][:, k * W:k * W + W],
                                                   ALU.mult, ALU.add).then_inc(s_acc, 1)
                    v.wait_ge(s_acc, n * PG + (k + 1))

            def attend(i):
                for q in range(NPART):
                    n = i * NPART + q
                    if part_before(i, q, 1):
                        maxima(*part_before(i, q, 1))
                        v.wait_ge(s_l, n)
                    b = load_blocks("B", i, q)
                    for k in range(PG):
                        a = nc.vector.tensor_copy(pair[:, k, :], nodes[:, bass.ds(b[k], 1), :].rearrange("p b c -> p (b c)"))
                    a.then_inc(s_pair, 1)
                    if part_before(i, q, 2):
                        add_weighted(*part_before(i, q, 2))
                    if part_after(i, q, 1):
                        masks(*part_after(i, q, 1))

            masks(0, 0)
            turns(v, ITERS, attend, last=1)
            maxima(ITERS - 1, NPART - 1)
            add_weighted(ITERS - 1, NPART - 2)
            add_weighted(ITERS - 1, NPART - 1)
            nc.vector.reciprocal(stat[:, 3, :], acc1[:, :, F]).then_inc(s_dve, 1)
            v.wait_ge(s_dve, nth())
            nc.vector.tensor_tensor(h_sb, acc1[:, :, 0:F], by_node(stat[:, 3, :]), ALU.mult).then_inc(s_dve, 1)
            v.wait_ge(s_dve, nth())
            nc.vector.scalar_tensor_tensor(x_sb, h_sb, 0.0, x_sb, ALU.max, ALU.add).then_inc(s_dve, 1)
            v.wait_ge(s_dve, nth())

            def plain(l, names):
                with v.Fori(0, ITERS) as i:
                    for q in range(NPART):
                        n = i * NPART + (l * NPP + q)
                        b = load_blocks(PASSES[l], i, q)
                        if PASSES[l] == "B":
                            name_targets(l, i, q)
                        else:
                            v.wait_ge(s_rec[q], i * LOADS[l] + (LOADED[l] + LOADS[l]))
                        ones_by_node(names[:, q, :], ALU.is_equal, q)
                        v.wait_ge(s_agg, n + 1)
                        add_sums(l, n, q, b)

            def add_sums(l, n, q, b):
                for k in range(PG):
                    here = acc[:, bass.ds(b[k], 1), :].rearrange("p b f -> p (b f)")
                    nc.vector.tensor_tensor(here, here, bank[4 + q % 2][:, k * F:k * F + F], ALU.add).then_inc(s_acc, 1)
                    v.wait_ge(s_acc, n * PG + (k + 1))

            layernorm()
            nc.vector.tensor_tensor(tmp, h_sb, by_node(dinv1[:, :]), ALU.mult).then_inc(s_dve, 1)
            v.wait_ge(s_dve, nth())
            nc.vector.tensor_copy(acc, tmp).then_inc(s_dve, 1)
            v.wait_ge(s_dve, nth())
            v.sem_inc(s_y, 1)
            plain(1, rec[:, :, :, A_LON])
            nc.vector.tensor_tensor(acc, acc, by_node(dinv1[:, :]), ALU.mult).then_inc(s_dve, 1)
            v.wait_ge(s_dve, nth())
            nc.vector.tensor_tensor(x_sb, x_sb, acc, ALU.add).then_inc(s_dve, 1)
            v.wait_ge(s_dve, nth())

            layernorm()
            nc.vector.tensor_tensor(tmp, h_sb, by_node(dinv2[:, :]), ALU.mult).then_inc(s_dve, 1)
            v.wait_ge(s_dve, nth())
            for l in range(2, LAST):
                nc.vector.memset(acc, 0.0).then_inc(s_dve, 1)
                v.wait_ge(s_dve, nth())
                v.sem_inc(s_y, 1)
                plain(l, recB[:, :, :, 0])
                nc.vector.tensor_tensor(acc, acc, by_node(dinv2[:, :]), ALU.mult).then_inc(s_dve, 1)
                v.wait_ge(s_dve, nth())
                nc.vector.tensor_tensor(h_sb, h_sb, acc, ALU.add).then_inc(s_dve, 1)
                v.wait_ge(s_dve, nth())
                nc.vector.tensor_tensor(tmp, acc, by_node(dinv2[:, :]), ALU.mult).then_inc(s_dve, 1)
                v.wait_ge(s_dve, nth())
            nc.vector.scalar_tensor_tensor(x_sb, h_sb, 0.25, x_sb, ALU.mult, ALU.add).then_inc(s_dve, 1)
            v.wait_ge(s_dve, nth())

            layernorm()
            nc.vector.memset(acc, 0.0).then_inc(s_dve, 1)
            v.wait_ge(s_dve, nth())
            v.sem_inc(s_m, 1)
            with v.Fori(0, NBLK // 2) as i:
                v.wait_ge(s_pr, i + 1)
                both = bank[1][:, 0:4 * F].rearrange("p (b k f) -> p b k f", b=2, k=2)
                nc.vector.tensor_copy(q_sb[:, bass.ds(i * 2, 2), :], both[:, :, 0, :])
                nc.vector.tensor_copy(tmp[:, bass.ds(i * 2, 2), :], both[:, :, 1, :]).then_inc(s_prc, 1)
            v.wait_ge(s_prc, NBLK // 2)
            v.sem_inc(s_y, 1)
            SCALE = float(D) ** -0.5

            def pair_ones(i, q):
                v.wait_ge(s_rec[q], i * 16 + (LOADED[LAST] + 16))
                ones_by_node(rec[:, q, :, A_LO], ALU.is_equal, q)

            def pairs(i):
                STEPS = 4
                for q in range(NPART):
                    n = i * NPART + q
                    v.wait_ge(s_gat[LAST // 3][q], i * (16 * PT) + (LAST % 3 * ITERS + 1) * 16 * PT)
                    nc.vector.tensor_tensor(msg2, rec[:, q, :, 0:F], gat[:, q, :, 0:F], ALU.mult).then_inc(s_m, 1)
                    v.wait_ge(s_m, n * STEPS + 2)
                    v.wait_ge(s_qg, n + 1)
                    nc.vector.tensor_tensor(msg2, msg2, bank[2][:, 0:PT * F].rearrange("p (t f) -> p t f", t=PT), ALU.mult).then_inc(s_m, 1)
                    v.wait_ge(s_m, n * STEPS + 3)
                    nc.vector.tensor_reduce(alpha[:, :, :], msg2.rearrange("p t (h d) -> p t h d", h=HEADS), AX.X, ALU.add).then_inc(s_m, 1)
                    v.wait_ge(s_m, n * STEPS + 4)
                    nc.vector.scalar_tensor_tensor(alpha[:, :, :], alpha[:, :, :], SCALE,
                                                   rec[:, q, :, A_PHI].unsqueeze(2).broadcast_to((P, PT, HEADS)),
                                                   ALU.mult, ALU.mult).then_inc(s_m, 1)
                    v.wait_ge(s_m, n * STEPS + 5)
                    nc.vector.tensor_tensor(msg[:, q % 2, :, :].rearrange("p t (h d) -> p t h d", h=HEADS),
                                            gat[:, q, :, F:2 * F].rearrange("p t (h d) -> p t h d", h=HEADS),
                                            alpha[:, :, :].unsqueeze(3).broadcast_to((P, PT, HEADS, D)), ALU.mult).then_inc(s_msg, 1)
                    if part_after(i, q, 2):
                        pair_ones(*part_after(i, q, 2))
                    if part_before(i, q, 1):
                        add_pairs(*part_before(i, q, 1))

            def add_pairs(i, q):
                n = i * NPART + (LAST * NPP + q)
                b = load_blocks("A", i, q)
                v.wait_ge(s_agg, n + 1)
                add_sums(LAST, n, q, b)

            pair_ones(0, 0)
            pair_ones(0, 1)
            turns(v, ITERS, pairs, first=1, last=1)
            add_pairs(ITERS - 1, NPART - 1)
            v.sem_inc(s_accd, 1)
            with v.Fori(0, NBLK // 2) as i:
                v.wait_ge(s_pr, i + (NBLK // 2 + 1))
                xs = x_sb[:, bass.ds(i * 2, 2), :]
                nc.vector.tensor_tensor(xs, xs, bank[1][:, 0:2 * F].rearrange("p (b f) -> p b f", b=2), ALU.add).then_inc(s_prc, 1)
            v.wait_ge(s_prc, NBLK)
            v.sem_inc(s_y, 1)


_INS = ["x", "src", "dst", "edge_attr_64", "edge_weight", "edge_weight_n2",
        "L0_gnn_w_i", "L0_gnn_w_j", "L3_gnn_Wq", "L3_gnn_Wk", "L3_gnn_Wv"]


def kernel(**inputs):
    import numpy as np
    import concourse.bacc as bacc
    from concourse import mybir as mb
    from concourse.bass_utils import run_bass_kernel_spmd

    nc = bacc.Bacc("TRN2", target_bir_lowering=False, num_devices=1)
    arrays, args = {}, []
    for name in _INS:
        a = np.ascontiguousarray(inputs[name])
        arrays[f"in_{name}"] = a
        args.append(nc.dram_tensor(f"in_{name}", a.shape, mb.dt.from_np(a.dtype), kind="ExternalInput").ap())
    args.append(nc.dram_tensor("out_x", inputs["x"].shape, mb.dt.float32, kind="ExternalOutput").ap())
    gnn_four_layers(nc, *args)
    r = run_bass_kernel_spmd(nc, [arrays], core_ids=[0])
    return r.results[0]["out_x"]
```
